# Optimizing a Trainium2 kernel written in Bass

```python
import numpy as np
import jax
import jax.numpy as jnp

def _softmax(x, axis=-1):
    return jax.nn.softmax(x, axis=axis)

def _gelu(x):
    return jax.nn.gelu(x, approximate=True)

def _silu(x):
    return jax.nn.silu(x)

def _sigmoid(x):
    return jax.nn.sigmoid(x)

def _layernorm(x, axis=-1, eps=1e-05):
    m = jnp.mean(x, axis=axis, keepdims=True)
    v = jnp.var(x, axis=axis, keepdims=True)
    return (x - m) / jnp.sqrt(v + eps)

def _scatter_add(tgt, idx, src, axis=0):
    return tgt.at[idx].add(src)

def _segment_sum(src, seg, n):
    return jax.ops.segment_sum(src, seg, n)
kernel_name = 'mk_audio_tower_d1_tok_aud1d512_r4_407ae9'

def setup_inputs(seed: int=0):
    np.random.seed(seed)
    _w = jnp.asarray

    def _rec_inputs():
        import jax
        import jax.numpy as jnp
        _rk = jax.random.key(seed)
        x = 0.000214012 + 1.00007 * jax.random.normal(jax.random.fold_in(_rk, 1), (16, 120000), jnp.float32)
        return x
    x = _rec_inputs()

    def _L0_tok_setup():
        import jax, jax.numpy as jnp
        import numpy as np
        HOP = 128

        def _dct_ortho_basis(n):
            k = np.arange(n)[:, None].astype(np.float64)
            t = np.arange(n)[None, :].astype(np.float64)
            D = np.cos(np.pi * (2.0 * t + 1.0) * k / (2.0 * n))
            scale = np.full((n, 1), np.sqrt(2.0 / n))
            scale[0, 0] = np.sqrt(1.0 / n)
            return jnp.asarray((scale * D).astype(np.float32))
        key = jax.random.key(seed)
        x = jax.random.normal(key, (32, 262000), dtype=jnp.float32)
        return {'x': x}
    _L0_tok_all = _L0_tok_setup()
    _L0_tok_in = {k: v for k, v in _L0_tok_all.items() if k in ()}
    del _L0_tok_all

    def _L0_attn_setup():
        import jax, jax.numpy as jnp
        import numpy as np
        B, T, C, H = (4, 256, 128, 4)
        D = C // H
        N_LAYER, LAYER_ID = (12, 1)

        def layernorm(x, g, b, eps=1e-05):
            m = x.mean(-1, keepdims=True)
            v = ((x - m) ** 2).mean(-1, keepdims=True)
            return g * (x - m) / jnp.sqrt(v + eps) + b

        def rmsnorm(x, scale, eps=1e-08):
            norm = jnp.sqrt(jnp.sum(x * x, axis=-1, keepdims=True)) / x.shape[-1] ** 0.5
            return scale * (x / (norm + eps))

        def lnssm_scan(q, k, v, lam):
            qT, kT, vT = (jnp.moveaxis(a, 1, 0) for a in (q, k, v))
            Bq = q.shape[0]
            A0 = jnp.zeros((Bq, q.shape[2], q.shape[3], q.shape[3]), q.dtype)
            z0 = jnp.zeros((Bq, q.shape[2], q.shape[3]), q.dtype)

            def step(carry, inp):
                A, z = carry
                qt, kt, vt = inp
                A = lam[None, :, :, None] * A + kt[..., None] * vt[..., None, :]
                z = lam[None] * z + kt
                St = jnp.einsum('bhi,bhij->bhj', qt, A)
                Zt = jnp.einsum('bhi,bhi->bh', qt, z)
                return ((A, z), (St, Zt))
            _, (S, Zs) = jax.lax.scan(step, (A0, z0), (qT, kT, vT))
            return (jnp.moveaxis(S, 0, 1), jnp.moveaxis(Zs, 0, 1))
        key = jax.random.key(seed)
        ks = jax.random.split(key, 10)
        w = lambda k, shape: 0.02 * jax.random.normal(k, shape, dtype=jnp.float32)
        r01 = LAYER_ID / (N_LAYER - 1)
        r1a0 = 1.0 - LAYER_ID / N_LAYER
        i = np.arange(C, dtype=np.float32)
        time_decay = (-5.0 + 8.0 * (i / (C - 1)) ** (0.7 + 1.3 * r01)).astype(np.float32)
        xv = i / C
        tm_q = (xv ** r1a0).astype(np.float32)[None, None, :]
        tm_k = (xv ** r1a0).astype(np.float32)[None, None, :]
        tm_v = (xv ** r1a0 + 0.3 * r01).astype(np.float32)[None, None, :]
        tm_g = (xv ** (0.5 * r1a0)).astype(np.float32)[None, None, :]
        return dict(x=jax.random.normal(ks[0], (B, T, C), dtype=jnp.float32), ln1_g=jnp.ones((C,), jnp.float32), ln1_b=jnp.zeros((C,), jnp.float32), ln2_g=jnp.ones((C,), jnp.float32), ln2_b=jnp.zeros((C,), jnp.float32), time_decay=jnp.asarray(time_decay), tm_q=jnp.asarray(tm_q), tm_k=jnp.asarray(tm_k), tm_v=jnp.asarray(tm_v), tm_g=jnp.asarray(tm_g), Wq=w(ks[1], (C, C)), Wk=w(ks[2], (C, C)), Wv=w(ks[3], (C, C)), Wg=w(ks[4], (C, C)), Wo=w(ks[5], (C, C)), rms_scale=jnp.ones((C,), jnp.float32), W1=w(ks[6], (4 * C, C)), W2=w(ks[7], (C, 4 * C)))
    _L0_attn_all = _L0_attn_setup()
    _L0_attn_in = {k: v for k, v in _L0_attn_all.items() if k in ('ln1_g', 'ln1_b', 'ln2_g', 'ln2_b', 'time_decay', 'tm_q', 'tm_k', 'tm_v', 'tm_g', 'Wq', 'Wk', 'Wv', 'Wg', 'Wo', 'rms_scale', 'W1', 'W2')}
    del _L0_attn_all

    def _L0_ffn_setup():
        import jax, jax.numpy as jnp
        import numpy as np
        MICRO_BATCHES = 2
        TOP_K = 2
        D = 128
        E = 8
        B, S = (8, 2048)
        key = jax.random.key(seed)
        ks = jax.random.split(key, 12)
        s = 0.02
        return {'x': jax.random.normal(ks[0], (B, S, D), dtype=jnp.float32), 'ln_g': jnp.ones((D,), jnp.float32), 'ln_b': jnp.zeros((D,), jnp.float32), 'attn_w': jax.random.normal(ks[1], (D, D), jnp.float32) * s, 'attn_b': jnp.zeros((D,), jnp.float32), 'gate_w': jax.random.normal(ks[2], (E, D), jnp.float32) * s, 'fc1_w': jax.random.normal(ks[3], (E, 4 * D, D), jnp.float32) * s, 'fc1_b': jnp.zeros((E, 4 * D), jnp.float32), 'fc2_w': jax.random.normal(ks[4], (E, D, 4 * D), jnp.float32) * s, 'fc2_b': jnp.zeros((E, D), jnp.float32), 'next_w': jax.random.normal(ks[5], (D, D), jnp.float32) * s, 'next_b': jnp.zeros((D,), jnp.float32)}
    _L0_ffn_all = _L0_ffn_setup()
    _L0_ffn_in = {k: v for k, v in _L0_ffn_all.items() if k in ('ln_g', 'ln_b', 'attn_w', 'attn_b', 'gate_w', 'fc1_w', 'fc1_b', 'fc2_w', 'fc2_b', 'next_w', 'next_b')}
    del _L0_ffn_all
    return {'x': x, 'L0_attn_ln1_g': _L0_attn_in['ln1_g'], 'L0_attn_ln1_b': _L0_attn_in['ln1_b'], 'L0_attn_ln2_g': _L0_attn_in['ln2_g'], 'L0_attn_ln2_b': _L0_attn_in['ln2_b'], 'L0_attn_time_decay': _L0_attn_in['time_decay'], 'L0_attn_tm_q': _L0_attn_in['tm_q'], 'L0_attn_tm_k': _L0_attn_in['tm_k'], 'L0_attn_tm_v': _L0_attn_in['tm_v'], 'L0_attn_tm_g': _L0_attn_in['tm_g'], 'L0_attn_Wq': _L0_attn_in['Wq'], 'L0_attn_Wk': _L0_attn_in['Wk'], 'L0_attn_Wv': _L0_attn_in['Wv'], 'L0_attn_Wg': _L0_attn_in['Wg'], 'L0_attn_Wo': _L0_attn_in['Wo'], 'L0_attn_rms_scale': _L0_attn_in['rms_scale'], 'L0_attn_W1': _L0_attn_in['W1'], 'L0_attn_W2': _L0_attn_in['W2'], 'L0_ffn_ln_g': _L0_ffn_in['ln_g'], 'L0_ffn_ln_b': _L0_ffn_in['ln_b'], 'L0_ffn_attn_w': _L0_ffn_in['attn_w'], 'L0_ffn_attn_b': _L0_ffn_in['attn_b'], 'L0_ffn_gate_w': _L0_ffn_in['gate_w'], 'L0_ffn_fc1_w': _L0_ffn_in['fc1_w'], 'L0_ffn_fc1_b': _L0_ffn_in['fc1_b'], 'L0_ffn_fc2_w': _L0_ffn_in['fc2_w'], 'L0_ffn_fc2_b': _L0_ffn_in['fc2_b'], 'L0_ffn_next_w': _L0_ffn_in['next_w'], 'L0_ffn_next_b': _L0_ffn_in['next_b']}

def reference(x, L0_attn_ln1_g, L0_attn_ln1_b, L0_attn_ln2_g, L0_attn_ln2_b, L0_attn_time_decay, L0_attn_tm_q, L0_attn_tm_k, L0_attn_tm_v, L0_attn_tm_g, L0_attn_Wq, L0_attn_Wk, L0_attn_Wv, L0_attn_Wg, L0_attn_Wo, L0_attn_rms_scale, L0_attn_W1, L0_attn_W2, L0_ffn_ln_g, L0_ffn_ln_b, L0_ffn_attn_w, L0_ffn_attn_b, L0_ffn_gate_w, L0_ffn_fc1_w, L0_ffn_fc1_b, L0_ffn_fc2_w, L0_ffn_fc2_b, L0_ffn_next_w, L0_ffn_next_b):
    import jax
    import jax.numpy as jnp

    def _L0_tok_ref(x):
        import jax, jax.numpy as jnp
        import numpy as np
        HOP = 128

        def _dct_ortho_basis(n):
            k = np.arange(n)[:, None].astype(np.float64)
            t = np.arange(n)[None, :].astype(np.float64)
            D = np.cos(np.pi * (2.0 * t + 1.0) * k / (2.0 * n))
            scale = np.full((n, 1), np.sqrt(2.0 / n))
            scale[0, 0] = np.sqrt(1.0 / n)
            return jnp.asarray((scale * D).astype(np.float32))
        x_len = x.shape[-1]
        pad_len = HOP - x_len % HOP
        x = jnp.pad(x, [(0, 0)] * (x.ndim - 1) + [(0, pad_len)])
        n_frames = x.shape[-1] // HOP
        frames = x.reshape(x.shape[:-1] + (n_frames, HOP))
        D = _dct_ortho_basis(HOP)
        return jnp.einsum('bfh,kh->bfk', frames, D)

    def _L0_attn_ref(x, ln1_g, ln1_b, ln2_g, ln2_b, time_decay, tm_q, tm_k, tm_v, tm_g, Wq, Wk, Wv, Wg, Wo, rms_scale, W1, W2):
        import jax, jax.numpy as jnp
        import numpy as np
        B, T, C, H = (4, 256, 128, 4)
        D = C // H
        N_LAYER, LAYER_ID = (12, 1)

        def layernorm(x, g, b, eps=1e-05):
            m = x.mean(-1, keepdims=True)
            v = ((x - m) ** 2).mean(-1, keepdims=True)
            return g * (x - m) / jnp.sqrt(v + eps) + b

        def rmsnorm(x, scale, eps=1e-08):
            norm = jnp.sqrt(jnp.sum(x * x, axis=-1, keepdims=True)) / x.shape[-1] ** 0.5
            return scale * (x / (norm + eps))

        def lnssm_scan(q, k, v, lam):
            qT, kT, vT = (jnp.moveaxis(a, 1, 0) for a in (q, k, v))
            Bq = q.shape[0]
            A0 = jnp.zeros((Bq, q.shape[2], q.shape[3], q.shape[3]), q.dtype)
            z0 = jnp.zeros((Bq, q.shape[2], q.shape[3]), q.dtype)

            def step(carry, inp):
                A, z = carry
                qt, kt, vt = inp
                A = lam[None, :, :, None] * A + kt[..., None] * vt[..., None, :]
                z = lam[None] * z + kt
                St = jnp.einsum('bhi,bhij->bhj', qt, A)
                Zt = jnp.einsum('bhi,bhi->bh', qt, z)
                return ((A, z), (St, Zt))
            _, (S, Zs) = jax.lax.scan(step, (A0, z0), (qT, kT, vT))
            return (jnp.moveaxis(S, 0, 1), jnp.moveaxis(Zs, 0, 1))
        Bx, Tx, Cx = x.shape
        Hh, Dd = (H, Cx // H)
        h = layernorm(x, ln1_g, ln1_b)
        xx = jnp.concatenate([jnp.zeros_like(h[:, :1]), h[:, :-1]], axis=1)
        xq = h * tm_q + xx * (1 - tm_q)
        xk = h * tm_k + xx * (1 - tm_k)
        xv_ = h * tm_v + xx * (1 - tm_v)
        xg = h * tm_g + xx * (1 - tm_g)
        q = xq @ Wq.T
        k = xk @ Wk.T
        v = xv_ @ Wv.T
        g = jax.nn.sigmoid(xg @ Wg.T)
        q = jnp.exp(rmsnorm(q, rms_scale))
        k = jnp.exp(rmsnorm(k, rms_scale))
        lam = jnp.exp(-jnp.exp(time_decay)).reshape(Hh, Dd)
        qh = q.reshape(Bx, Tx, Hh, Dd)
        kh = k.reshape(Bx, Tx, Hh, Dd)
        vh = v.reshape(Bx, Tx, Hh, Dd)
        S, Zs = lnssm_scan(qh, kh, vh, lam)
        att = (S / Zs[..., None]).reshape(Bx, Tx, Cx)
        att = g * att @ Wo.T
        x = x + att
        h2 = layernorm(x, ln2_g, ln2_b)
        x = x + jax.nn.gelu(h2 @ W1.T, approximate=False) @ W2.T
        return x

    def _L0_ffn_ref(x, ln_g, ln_b, attn_w, attn_b, gate_w, fc1_w, fc1_b, fc2_w, fc2_b, next_w, next_b):
        import jax, jax.numpy as jnp
        import numpy as np
        MICRO_BATCHES = 2
        TOP_K = 2
        D = 128
        E = 8
        B, S = (8, 2048)
        b, s, d = x.shape
        xf = x.reshape(b * s, d)
        mu = jnp.mean(xf, axis=-1, keepdims=True)
        var = jnp.var(xf, axis=-1, keepdims=True)
        normed = (xf - mu) / jnp.sqrt(var + 1e-05) * ln_g + ln_b
        x_attn = normed @ attn_w.T + attn_b + xf
        logits = x_attn @ gate_w.T
        _scores, _indices = jax.lax.top_k(logits, TOP_K)
        e = fc1_w.shape[0]
        t = b * s // (MICRO_BATCHES * e)
        tok = x_attn.reshape(MICRO_BATCHES, e, t, d)
        h = jnp.einsum('meti,ehi->meth', tok, fc1_w) + fc1_b[None, :, None, :]
        h = jax.nn.gelu(h, approximate=False)
        y = jnp.einsum('meth,edh->metd', h, fc2_w) + fc2_b[None, :, None, :]
        yf = y.reshape(b * s, d)
        out = jax.nn.gelu(yf @ next_w.T + next_b, approximate=False)
        return out.reshape(b, s, d)
    h = _L0_tok_ref(x)
    h = h + _L0_attn_ref(_layernorm(h, axis=-1), L0_attn_ln1_g, L0_attn_ln1_b, L0_attn_ln2_g, L0_attn_ln2_b, L0_attn_time_decay, L0_attn_tm_q, L0_attn_tm_k, L0_attn_tm_v, L0_attn_tm_g, L0_attn_Wq, L0_attn_Wk, L0_attn_Wv, L0_attn_Wg, L0_attn_Wo, L0_attn_rms_scale, L0_attn_W1, L0_attn_W2)
    h = h + _L0_ffn_ref(_layernorm(h, axis=-1), L0_ffn_ln_g, L0_ffn_ln_b, L0_ffn_attn_w, L0_ffn_attn_b, L0_ffn_gate_w, L0_ffn_fc1_w, L0_ffn_fc1_b, L0_ffn_fc2_w, L0_ffn_fc2_b, L0_ffn_next_w, L0_ffn_next_b)
    return h

_drawn_inputs = setup_inputs


def setup_inputs(seed=0):
    import zlib

    import numpy as np

    out = dict(_drawn_inputs(seed))
    spreads = {'L0_attn_ln1_g': (1.0, 0.6),
     'L0_attn_ln1_b': (0.0, 0.8),
     'L0_attn_ln2_g': (1.0, 0.6),
     'L0_attn_ln2_b': (0.0, 2.0),
     'L0_attn_rms_scale': (1.0, 0.6),
     'L0_ffn_ln_g': (1.0, 0.6),
     'L0_ffn_ln_b': (0.0, 0.8),
     'L0_ffn_attn_b': (0.0, 0.8),
     'L0_ffn_fc1_b': (0.0, 0.8),
     'L0_ffn_fc2_b': (0.0, 0.8),
     'L0_ffn_next_b': (0.0, 2.0)}
    factors = {'L0_attn_time_decay': 8.0,
     'L0_attn_tm_q': 8.0,
     'L0_attn_tm_k': 8.0,
     'L0_attn_tm_v': 8.0,
     'L0_attn_tm_g': 8.0,
     'L0_attn_Wq': 8.0,
     'L0_attn_Wk': 8.0,
     'L0_attn_Wv': 7.549,
     'L0_attn_Wg': 8.0,
     'L0_attn_Wo': 7.582,
     'L0_ffn_attn_w': 8.0,
     'L0_ffn_fc1_w': 8.0,
     'L0_ffn_fc2_w': 8.0,
     'L0_ffn_next_w': 8.0,
     'L0_attn_W1': 6.835,
     'L0_attn_W2': 6.83}
    for name, (base, spread) in spreads.items():
        noise = np.random.default_rng([zlib.crc32(name.encode()), seed]).standard_normal(out[name].shape)
        drawn = base * np.exp(spread * noise) if base else spread * noise
        out[name] = jnp.asarray(drawn.astype(out[name].dtype))
    for name, factor in factors.items():
        out[name] = (out[name] * factor).astype(out[name].dtype)
    return out
```

```python
import concourse.bass as bass
from concourse import mybir
from contextlib import ExitStack

F32 = mybir.dt.float32
U32 = mybir.dt.uint32
ALU = mybir.AluOpType
ACT = mybir.ActivationFunctionType

P = 128
HEADS = 4
HD = P // HEADS
WIN = 32
HALF = 512
EPS = 1e-5
EIGHT, FOUR = 8, 4
NW, NE = P // WIN, WIN // EIGHT
Q8, Q32, Q4 = HALF, 2 * HALF, 3 * HALF
QCOLS = 3 * HALF + HALF // 2
SW = HEADS * WIN

FRONT = ["dct0", "dct1", "nT0", "nT1", "q0", "q1", "k0", "k1", "v0", "v1", "g0", "g1",
         "qT0", "qT1", "kT0", "kT1", "kc0", "kc1", "z0", "z1", "u0", "u1"]
MLP = (["wo0", "wo1", "n2T0"] + [f"w1_0{j}" for j in range(4)] + ["n2T1"]
       + [f"w1_1{j}" for j in range(4)] + ["w2_0", "w2_1", "n1T0", "nmT0", "at0"]
       + [f"f1_0{j}" for j in range(4)] + ["n1T1", "nmT1", "at1", "f2_0", "oT0"]
       + [f"f1_1{j}" for j in range(4)] + ["f2_1", "oT1"])


def pair_mask():
    import numpy as np
    s = np.arange(P)[:, None] % WIN
    t = np.arange(WIN)[None, :]
    half = t[:, t[0] % EIGHT >= FOUR]
    cols = [(s // FOUR == t // FOUR) & (s <= t)] * HEADS
    cols += [(s // EIGHT == half // EIGHT) & (s % EIGHT < FOUR)] * HEADS
    return np.concatenate(cols, axis=1).astype(np.uint32)


def dct_basis():
    import numpy as np
    k = np.arange(P)[:, None].astype(np.float64)
    t = np.arange(P)[None, :].astype(np.float64)
    scale = np.full((P, 1), np.sqrt(2.0 / P))
    scale[0, 0] = np.sqrt(1.0 / P)
    return np.ascontiguousarray((scale * np.cos(np.pi * (2.0 * t + 1.0) * k / (2.0 * P))).astype(np.float32).T)


def program(nc, A, out):
    B, _, full = A["xT"].shape
    T = full + 1
    TAIL = A["xtail"].shape[1]
    E = A["fc1T"].shape[0]
    TILES = -(-T // P)
    PADT = TILES * P
    WINS = -(-T // WIN)
    last_rows = T - (TILES - 1) * P
    width = [HALF, T - HALF]
    scan_w = [HALF, WINS * WIN - HALF]
    windows = [min(4, WINS - 4 * c) for c in range(TILES)]
    NST = TILES - 1

    ctx = ExitStack()
    with ctx:
        def sb(name, *shape, dt=F32):
            return ctx.enter_context(nc.sbuf_tensor(name, [P, *shape], dt))

        def sem(name):
            return ctx.enter_context(nc.semaphore(name))

        ident, heads1, dct = sb("ident", P), sb("heads1", P), sb("dct", P)
        mask = sb("mask", SW + SW // 2, dt=U32)
        wq, wk, wv, wg, wo, wat, wnext = (sb(n, P) for n in ("wq", "wk", "wv", "wg", "wo", "wat", "wnext"))
        w1 = sb("w1", 4 * P)
        w2 = sb("w2", 4, P)
        vec = sb("vec", 16)
        VEC = {n: i for i, n in enumerate(
            ["ln1_g", "ln1_b", "ln2_g", "ln2_b", "td", "tm_q", "tm_k", "tm_v", "tm_g", "rms", "f_g", "f_b",
             "at_b", "nx_b"])}
        col = lambda n: vec[:, VEC[n]:VEC[n] + 1]
        fc2b = sb("fc2b", E)
        lam = sb("lam", 2)
        pw = sb("pw", P + 1)
        rp = sb("rp", P + 1)
        zeros = sb("zeros", P)
        tick = sb("tick", 1)
        nhalf = sb("nhalf", 8)
        phalf = sb("phalf", 8)
        f1w = sb("f1w", 4 * P)
        f2w = sb("f2w", 4 * P + 1)
        f1b = sb("f1b", 4)
        g_dram = nc.dram_tensor("g_dram", [E, P, 4 * P + 1], F32, kind="Internal").ap()

        xT = sb("xT", PADT)
        h = sb("h", TILES, P)
        nl = sb("nl", TILES, P)
        st1 = sb("st1", TILES, 6)
        mv1, vv1, rr1 = sb("mv1", TILES, 2), sb("vv1", TILES, 2), sb("rr1", TILES, 2)
        hl = sb("hl", PADT + 1)
        d = sb("d", PADT)
        xq, xk, xv, xg = (sb(n, PADT) for n in ("xq", "xk", "xv", "xg"))
        z, qz, th, gz = d, xv, xq, xk
        qk = [sb("qtok", TILES, P), sb("ktok", TILES, P)]
        ssq, nrm, rin = sb("ssq", 2, TILES), sb("nrm", 2, TILES), sb("rin", 2, TILES)
        v = sb("v", TILES, P)
        q, k = sb("q", PADT), sb("k", PADT)
        ql = sb("ql", QCOLS - HALF)
        qx = sb("qx", HEADS, QCOLS)
        ki, kh, ko, kw = sb("ki", FOUR - 1, HALF), sb("kh", HALF), sb("ko", NE - 1, HALF), sb("kw", NW - 1, HALF)
        kc, kcT = sb("kc", NST * P), sb("kcT", NST, P)
        qc = sb("qc", PADT)
        af, ab = sb("af", NST, P), sb("ab", NST, P)
        pd = [sb(f"pd{i}", HEADS * WIN) for i in range(2)]
        px = [sb(f"px{i}", HEADS, P) for i in range(2)]
        ga = sb("ga", PADT)
        a_out, h_out = sb("a_out", TILES, P), sb("h_out", TILES, P)

        x2, nl2, t = sb("x2", TILES, P), sb("nl2", TILES, P), sb("t", TILES, P)
        st2, mv2, vv2, rr2 = sb("st2", TILES, 6), sb("mv2", TILES, 2), sb("vv2", TILES), sb("rr2", TILES)
        st3, mv3, vv3, rr3 = sb("st3", TILES, 6), sb("mv3", TILES, 2), sb("vv3", TILES, 2), sb("rr3", TILES, 2)
        h1, n1, n2 = t, nl2, x2
        c1, xa = sb("c1", PADT), sb("xa", PADT)
        hid = sb("hid", 4, PADT)

        bank = [ctx.enter_context(nc.psum_tensor(f"bank{i}", [P, 512], F32)) for i in range(8)]

        s_w = sem("s_w"); s_fc2 = sem("s_fc2"); s_zero = sem("s_zero"); s_init = sem("s_init")
        s_gp = sem("s_gp"); s_gc = sem("s_gc"); s_gd = sem("s_gd"); s_lam = sem("s_lam"); s_pw = sem("s_pw")
        s_tab = sem("s_tab")
        x_in = sem("x_in")
        e_in = sem("e_in")
        qx_in = sem("qx_in")
        o_out = sem("o_out")
        front = sem("front")
        mlp = sem("mlp")
        diag = sem("diag")
        off = sem("off")
        s_out = sem("s_out")
        h_cp = sem("h_cp"); hl_ok = sem("hl_ok")
        raw = sem("raw")
        v_ok = sem("v_ok"); th_ok = sem("th_ok"); eq = sem("eq"); ek = sem("ek"); kcT_ok = sem("kcT_ok")
        px_ok = sem("px_ok")
        hh_ok = sem("hh_ok")
        n2T_ok = sem("n2T_ok"); n1T_ok = sem("n1T_ok"); nmT_ok = sem("nmT_ok"); fin_ok = sem("fin_ok")
        ge1 = sem("ge1"); ge2 = sem("ge2")
        bn1 = sem("bn1"); ag1 = sem("ag1"); var1 = sem("var1"); nl_ok = sem("nl_ok")
        mix = sem("mix")
        nr_ok = sem("nr_ok"); ri_ok = sem("ri_ok")
        tok = sem("tok")
        ql_ok = sem("ql_ok")
        kc_ok = sem("kc_ok"); qc_ok = sem("qc_ok"); z_ok = sem("z_ok"); qz_ok = sem("qz_ok")
        af_ok = sem("af_ok")
        rz_ok = sem("rz_ok"); gz_ok = sem("gz_ok"); ga_ok = sem("ga_ok")
        pd_ok = sem("pd_ok"); merged = sem("merged")
        aa_ok = sem("aa_ok")
        x2_ok = sem("x2_ok"); bn2 = sem("bn2"); ag2 = sem("ag2"); var2 = sem("var2"); nl2_ok = sem("nl2_ok")
        h1_ok = sem("h1_ok"); bn3 = sem("bn3"); ag3 = sem("ag3"); var3 = sem("var3"); n12_ok = sem("n12_ok")
        xa_ok = sem("xa_ok"); y_ok = sem("y_ok")
        r1_ok = sem("r1_ok"); rq_ok = sem("rq_ok"); r2_ok = sem("r2_ok"); r3_ok = sem("r3_ok"); t_ok = sem("t_ok")
        d_ok = sem("d_ok"); ab_ok = sem("ab_ok")
        kl_ok = sem("kl_ok")

        def nth(b, per, n):
            return b * per + n

        def before(eng, s, b, per, n):
            if not (isinstance(b, int) and b == 0):
                eng.wait_ge(s, (b - 1) * per + n)

        emptied = {}
        for g in (0, 1):
            for name, s in (("dct", h_cp), ("nT", hl_ok), ("v", v_ok), ("g", th_ok), ("qT", eq), ("kT", ek),
                            ("kc", kcT_ok), ("z", rz_ok)):
                emptied[f"{name}{g}"] = (s, 2, g + 1)
            emptied[f"q{g}"] = (raw, 4, g + 1)
            emptied[f"k{g}"] = (raw, 4, g + 3)
            for name, s in (("wo", x2_ok), ("n2T", n2T_ok), ("w2_", h1_ok), ("n1T", n1T_ok), ("nmT", nmT_ok),
                            ("at", xa_ok), ("f2_", fin_ok), ("oT", y_ok)):
                emptied[f"{name}{g}"] = (s, 2, g + 1)
            for j in range(4):
                emptied[f"w1_{g}{j}"] = (ge1, 8, 4 * g + j + 1)
                emptied[f"f1_{g}{j}"] = (ge2, 8, 4 * g + j + 1)
        emptied["u0"] = (af_ok, NST, 4)
        emptied["u1"] = (af_ok, NST, NST)

        def front_bank(pe, b, name):
            n = FRONT.index(name)
            if n >= 4:
                s, per, i = emptied[FRONT[n - 4]]
                pe.wait_ge(s, nth(b, per, i))
            elif name == "dct0":
                before(pe, pd_ok, b, TILES, TILES - 1)
            elif name == "dct1":
                before(pe, pd_ok, b, TILES, TILES)
            elif name == "nT0":
                before(pe, px_ok, b, TILES, TILES)
            else:
                before(pe, ga_ok, b, 2, 2)
            return bank[n % 4]

        def mlp_bank(pe, b, name):
            n = MLP.index(name)
            if n >= 4:
                s, per, i = emptied[MLP[n - 4]]
                pe.wait_ge(s, nth(b, per, i))
            else:
                s, per, i = emptied[MLP[len(MLP) - 4 + n]]
                before(pe, s, b, per, i)
            return bank[4 + n % 4]

        def used(b, name):
            return nth(b, len(FRONT), FRONT.index(name) + 1)

        def used_b(b, name):
            return nth(b, len(MLP), MLP.index(name) + 1)

        def bf(name):
            return bank[FRONT.index(name) % 4]

        def bm(name):
            return bank[4 + MLP.index(name) % 4]

        def cols(g):
            return slice(HALF * g, HALF * g + width[g])

        def tiles(g):
            return range(4 * g, 4 * g + 4)

        def over(ap, n, m):
            return ap.rearrange("p (o m) -> p o m", o=1).to_broadcast([P, n, m])

        block = ctx.enter_context(nc.Block())

        @block.sync
        def _(sp):
            loads = [(ident, A["ident"]), (heads1, A["heads1"]), (dct, A["dct"]), (mask, A["mask"]),
                     (wq, A["wqT"]), (wk, A["wkT"]), (wv, A["wvT"]), (wg, A["wgT"]), (wo, A["woT"]),
                     (wat, A["watT"]), (wnext, A["wnextT"]), (w1, A["w1T"]), (fc2b, A["fc2bT"])]
            sp.dma_start(hid[:, :, :].rearrange("p j (a n) -> p (j a) n", a=2), A["fc2"].rearrange("e d n -> d e n")).then_inc(s_fc2, 16)
            for dst, src in loads:
                sp.dma_start(dst[:, :], src).then_inc(s_w, 16)
            sp.dma_start(w2[:, :, :], A["w2T"].rearrange("(j p) n -> p j n", p=P)).then_inc(s_w, 16)
            for name, i in VEC.items():
                sp.dma_start(vec[:, i:i + 1], A[name].rearrange("(p o) -> p o", o=1)).then_inc(s_w, 16)

            def samples(b):
                if not (isinstance(b, int) and b == 0):
                    sp.wait_ge(front, used(b - 1, "dct1"))
                sp.dma_start(xT[:, 0:full], A["xT"][b, :, :]).then_inc(x_in, 16)
                sp.dma_start(xT[0:TAIL, full:T], A["xtail"][b, :].rearrange("(p o) -> p o", o=1)).then_inc(x_in, 16)

            sp.wait_ge(s_zero, 1)
            samples(0)
            sp.wait_ge(s_gc, E + 1)
            G = qx[:, :, :].rearrange("p h n -> p (h n)")[:, 0:E * (4 * P + 1)].rearrange("p (e n) -> p e n", e=E)
            sp.dma_start(g_dram.rearrange("e p n -> p e n"), G).then_inc(s_gd, 16)
            sp.wait_ge(s_gd, 16)

            def expert(p):
                e = p % E
                before(sp, mlp, p, len(MLP), MLP.index("f2_1") + 1)
                before(sp, fin_ok, p, 2, 2)
                sp.dma_start(f1w[:, :], A["fc1T"][e, :, :]).then_inc(e_in, 16)
                sp.dma_start(f1b[:, :], A["fc1b"][e, :, :]).then_inc(e_in, 16)
                sp.dma_start(f2w[:, :], g_dram[e, :, :]).then_inc(e_in, 16)

            def spread(b, g):
                if g:
                    sp.wait_ge(off, nth(b, TILES, 4))
                else:
                    before(sp, off, b, TILES, TILES)
                    if isinstance(b, int) and b == 0:
                        sp.wait_ge(s_init, 1)
                if g == 0:
                    sp.wait_ge(eq, nth(b, 2, 2))
                for hd in range(HEADS):
                    rows = slice(HD * hd, HD * hd + HD)
                    sp.dma_start(qx[rows, hd, 0:scan_w[g]], q[rows, HALF * g:HALF * g + scan_w[g]]).then_inc(qx_in, 16)
                sp.wait_ge(ql_ok, nth(b, 2, g + 1))
                for hd in range(HEADS):
                    rows = slice(HD * hd, HD * hd + HD)
                    sp.dma_start(qx[rows, hd, HALF:QCOLS], ql[rows, :]).then_inc(qx_in, 16)

            def store(p, g):
                sp.wait_ge(y_ok, nth(p, 2, g + 1))
                r0 = HALF * g
                whole = 4 - g
                sp.dma_start(out[p, r0:r0 + whole * P, :].rearrange("(m p) n -> p m n", p=P),
                             h1[:, 4 * g:4 * g + whole, :]).then_inc(o_out, 16)
                if g:
                    sp.dma_start(out[p, (TILES - 1) * P:T, :], h1[0:last_rows, TILES - 1, :]).then_inc(o_out, 16)

            def body(a, p):
                if p is not None:
                    expert(p)
                if a is not None and not (isinstance(a, int) and a == 0):
                    samples(a)
                if a is not None:
                    spread(a, 0)
                    spread(a, 1)
                if p is not None:
                    store(p, 0)
                    store(p, 1)
            body(0, None)
            body(1, 0)
            with sp.Fori(2, B) as i:
                body(i, i - 1)
            body(None, B - 1)
            sp.wait_ge(o_out, 48 * B)

        @block.gpsimd
        def _(gp):
            gp.memset(xT[:, :], 0.0).then_inc(s_zero, 1)
            for tile in (nhalf, phalf):
                gp.memset(tile[:, :], -0.5 if tile is nhalf else 0.5)
            for tile in (xq, xk, xv, xg, q, k, ga, hl, kh, pd[0], pd[1]):
                gp.memset(tile[:, :], 0.0)
            for tile in (ki, ko, kw, px[0], px[1]):
                gp.memset(tile[:, :, :], 0.0)
            gp.memset(ql[:, :], 0.0)
            gp.wait_ge(s_fc2, 16)
            gp.wait_ge(s_gc, E)
            gp.memset(hid[:, :, :], 0.0)
            gp.memset(c1[:, :], 0.0)
            gp.memset(xa[:, :], 0.0)
            gp.wait_ge(s_gd, 16)
            gp.memset(qx[:, :, :], 0.0).then_inc(s_init, 1)
            gp.wait_ge(s_tab, 1)

            def pow1(a, g):
                gp.wait_ge(var1, nth(a, 2, g + 1))
                gp.tensor_tensor(rr1[:, 4 * g:4 * g + 4, :], vv1[:, 4 * g:4 * g + 4, :],
                                 nhalf[:, 0:8].rearrange("p (m o) -> p m o", o=2), ALU.pow).then_inc(r1_ok, 1)

            def diff(a):
                gp.wait_ge(hl_ok, nth(a, 2, 2))
                gp.tensor_tensor(d[:, 0:T], hl[:, 1:T + 1], hl[:, 0:T], ALU.subtract).then_inc(d_ok, 1)

            def powq(a, i):
                gp.wait_ge(raw, nth(a, 4, 2 * i + 2))
                gp.tensor_tensor(nrm[:, i, :], ssq[:, i, :], phalf[:, 0:TILES], ALU.pow).then_inc(rq_ok, 1)

            def klev(a, g):
                gp.wait_ge(ek, nth(a, 2, g + 1))
                if g:
                    gp.wait_ge(off, nth(a, TILES, 4))
                else:
                    before(gp, off, a, TILES, TILES)
                parts = [(ki[:, j - 1, :], FOUR, j + 1, j) for j in range(1, FOUR)]
                parts += [(kh[:, :], EIGHT, FOUR, FOUR)]
                parts += [(ko[:, j - 1, :], WIN, EIGHT * j, EIGHT * j) for j in range(1, NE)]
                parts += [(kw[:, w - 1, :], P, WIN * w, WIN * w) for w in range(1, NW)]
                for dst, m, n, b in parts:
                    w = scan_w[g] // m * m
                    if m == P and w < scan_w[g]:
                        w = HALF
                    view = lambda ap: ap.rearrange("p (x m) -> p x m", m=m)[:, :, 0:n]
                    last = gp.tensor_tensor(view(dst[:, 0:w]), view(k[:, HALF * g:HALF * g + w]),
                                            over(rp[:, P - b:P - b + n], w // m, n), ALU.mult)
                last.then_inc(kl_ok, 1)

            def states(a):
                gp.wait_ge(af_ok, nth(a, NST, NST))
                gp.tensor_tensor(ab[:, :, :], af[:, :, :], over(heads1[:, :], NST, P), ALU.mult).then_inc(ab_ok, 1)

            def pow2(p, g):
                gp.wait_ge(var2, nth(p, 2, g + 1))
                gp.tensor_tensor(rr2[:, 4 * g:4 * g + 4], vv2[:, 4 * g:4 * g + 4], nhalf[:, 0:4], ALU.pow).then_inc(r2_ok, 1)

            def resid(p, g):
                before(gp, o_out, p, 48, 48)
                gp.wait_ge(x2_ok, nth(p, 2, g + 1))
                gp.wait_ge(hh_ok, nth(p, 1, 1))
                gp.tensor_tensor(t[:, 4 * g:4 * g + 4, :], x2[:, 4 * g:4 * g + 4, :], h_out[:, 4 * g:4 * g + 4, :],
                                 ALU.add).then_inc(t_ok, 1)

            def pow3(p, g):
                gp.wait_ge(var3, nth(p, 2, g + 1))
                gp.tensor_tensor(rr3[:, 4 * g:4 * g + 4, :], vv3[:, 4 * g:4 * g + 4, :],
                                 nhalf[:, 0:8].rearrange("p (m o) -> p m o", o=2), ALU.pow).then_inc(r3_ok, 1)

            def body(a, p):
                if a is not None:
                    pow1(a, 0); pow1(a, 1)
                if p is not None:
                    pow2(p, 0); pow2(p, 1); resid(p, 0); resid(p, 1)
                if a is not None:
                    diff(a); powq(a, 0); powq(a, 1)
                if p is not None:
                    pow3(p, 0); pow3(p, 1)
                if a is not None:
                    klev(a, 0); states(a); klev(a, 1)
            body(0, None)
            body(1, 0)
            with gp.Fori(2, B) as i:
                body(i, i - 1)
            body(None, B - 1)

        @block.scalar
        def _(act):
            G = qx[:, :, :].rearrange("p h n -> p (h n)")[:, 0:E * (4 * P + 1)].rearrange("p (e n) -> p e n", e=E)
            for e in range(E):
                act.wait_ge(s_gp, e + 1)
                nc.scalar.activation(G[:, e, 0:4 * P], bank[e][:, :], ACT.Copy).then_inc(s_gc, 1)
            act.wait_ge(s_gp, E + 1)
            nc.scalar.activation(G[:, :, 4 * P], bank[0][:, 0:E], ACT.Identity, bias=col("nx_b")).then_inc(s_gc, 1)
            act.wait_ge(s_w, 28 * 16)
            nc.scalar.activation(lam[:, 0:1], col("td"), ACT.Exp).then_inc(s_lam, 1)
            act.wait_ge(s_lam, 1)
            nc.scalar.activation(lam[:, 1:2], lam[:, 0:1], ACT.Exp, scale=-1.0).then_inc(s_lam, 1)

            def hcopy(a, g):
                act.wait_ge(front, used(a, f"dct{g}"))
                before(act, hh_ok, a, 1, 1)
                before(act, aa_ok, a, 1, 1)
                nc.scalar.activation(h[:, 4 * g:4 * g + 4, :], bf(f"dct{g}")[:, :].rearrange("p (m n) -> p m n", m=4), ACT.Copy).then_inc(h_cp, 1)

            def hlT(a, g):
                act.wait_ge(front, used(a, f"nT{g}"))
                if g == 0:
                    before(act, mix, a, 4, 4)
                nc.scalar.activation(hl[:, 1 + HALF * g:1 + HALF * g + width[g]], bf(f"nT{g}")[:, 0:width[g]], ACT.Identity,
                                     scale=col("ln1_g"), bias=col("ln1_b")).then_inc(hl_ok, 1)

            def squares(a, i, g):
                name = f"{'qk'[i]}{g}"
                junk = (q, k)[i]
                act.wait_ge(front, used(a, name))
                nc.scalar.activation(qk[i][:, 4 * g:4 * g + 4, :], bf(name)[:, :].rearrange("p (m n) -> p m n", m=4), ACT.Copy)
                for m in range(4):
                    last = nc.scalar.activation(junk[:, P * (4 * g + m):P * (4 * g + m) + P], bf(name)[:, P * m:P * m + P], ACT.Square,
                                                accum_out=ssq[:, i, 4 * g + m:4 * g + m + 1])
                last.then_inc(raw, 1)

            def vcopy(a, g):
                act.wait_ge(front, used(a, f"v{g}"))
                nc.scalar.activation(v[:, 4 * g:4 * g + 4, :], bf(f"v{g}")[:, :].rearrange("p (m n) -> p m n", m=4), ACT.Copy).then_inc(v_ok, 1)

            def gate(a, g):
                act.wait_ge(front, used(a, f"g{g}"))
                nc.scalar.activation(th[:, cols(g)], bf(f"g{g}")[:, 0:width[g]], ACT.Tanh, scale=0.5).then_inc(th_ok, 1)

            def exps(a, i, g):
                name = f"{'qk'[i]}T{g}"
                act.wait_ge(front, used(a, name))
                nc.scalar.activation((q, k)[i][:, cols(g)], bf(name)[:, 0:width[g]], ACT.Exp,
                                     scale=col("rms")).then_inc((eq, ek)[i], 1)

            def kcopy(a, g):
                n = (4, NST - 4)[g]
                act.wait_ge(front, used(a, f"kc{g}"))
                nc.scalar.activation(kcT[:, 4 * g:4 * g + n, :], bf(f"kc{g}")[:, 0:P * n].rearrange("p (m n) -> p m n", m=n), ACT.Copy).then_inc(kcT_ok, 1)

            def pxs(a, c):
                X, O, n = px[c % 2], bank[2], windows[c]
                if c >= 2:
                    act.wait_ge(s_out, nth(a, TILES, c - 1))
                else:
                    before(act, s_out, a, TILES, TILES - 1 + c)
                act.wait_ge(off, nth(a, TILES, c + 1))
                for w in range(1, n):
                    nc.scalar.activation(X[0:WIN * w, :, WIN * w:WIN * w + WIN],
                                         O[0:WIN * w, SW * (w - 1):SW * w].rearrange("p (h n) -> p h n", h=HEADS), ACT.Copy)
                act.wait_ge(pd_ok, nth(a, TILES, c + 1))
                for w in range(n):
                    r = slice(WIN * w, WIN * w + WIN)
                    last = nc.scalar.activation(X[r, :, r], pd[c % 2][r, :].rearrange("p (h n) -> p h n", h=HEADS), ACT.Copy)
                last.then_inc(px_ok, 1)

            def hand(a):
                before(act, t_ok, a, 2, 2)
                nc.scalar.activation(h_out[:, :, :], h[:, :, :], ACT.Copy).then_inc(hh_ok, 1)

            def n2T(p, g):
                act.wait_ge(mlp, used_b(p, f"n2T{g}"))
                nc.scalar.activation(c1[:, cols(g)], bm(f"n2T{g}")[:, 0:width[g]], ACT.Identity,
                                     scale=col("ln2_g"), bias=col("ln2_b")).then_inc(n2T_ok, 1)

            def gelu1(p, g):
                for j in range(4):
                    act.wait_ge(mlp, used_b(p, f"w1_{g}{j}"))
                    nc.scalar.activation(hid[:, j, cols(g)], bm(f"w1_{g}{j}")[:, 0:width[g]], ACT.Gelu).then_inc(ge1, 1)

            def nT(p, g):
                act.wait_ge(mlp, used_b(p, f"n1T{g}"))
                nc.scalar.activation(xa[:, cols(g)], bm(f"n1T{g}")[:, 0:width[g]], ACT.Copy).then_inc(n1T_ok, 1)
                act.wait_ge(mlp, used_b(p, f"nmT{g}"))
                nc.scalar.activation(c1[:, cols(g)], bm(f"nmT{g}")[:, 0:width[g]], ACT.Identity,
                                     scale=col("f_g"), bias=col("f_b")).then_inc(nmT_ok, 1)

            def gelu2(p, g):
                act.wait_ge(e_in, nth(p, 48, 48))
                for j in range(4):
                    act.wait_ge(mlp, used_b(p, f"f1_{g}{j}"))
                    nc.scalar.activation(hid[:, j, cols(g)], bm(f"f1_{g}{j}")[:, 0:width[g]], ACT.Gelu,
                                         bias=f1b[:, j:j + 1]).then_inc(ge2, 1)

            def fin(p, g):
                act.wait_ge(mlp, used_b(p, f"f2_{g}"))
                nc.scalar.activation(c1[:, cols(g)], bm(f"f2_{g}")[:, 0:width[g]], ACT.Gelu,
                                     bias=f2w[:, 4 * P:4 * P + 1]).then_inc(fin_ok, 1)

            def body(a, p):
                if a is not None:
                    hcopy(a, 0); hcopy(a, 1); hlT(a, 0); hlT(a, 1)
                if p is not None:
                    n2T(p, 0); gelu1(p, 0)
                if a is not None:
                    for i in (0, 1):
                        squares(a, i, 0); squares(a, i, 1)
                if p is not None:
                    n2T(p, 1); gelu1(p, 1)
                if a is not None:
                    vcopy(a, 0); vcopy(a, 1); gate(a, 0); gate(a, 1)
                    exps(a, 0, 0); exps(a, 0, 1); exps(a, 1, 0); exps(a, 1, 1)
                if p is not None:
                    nT(p, 0)
                if a is not None:
                    kcopy(a, 0); kcopy(a, 1)
                if p is not None:
                    gelu2(p, 0)
                if a is not None:
                    for c in range(4):
                        pxs(a, c)
                if p is not None:
                    nT(p, 1); fin(p, 0); gelu2(p, 1)
                if a is not None:
                    pxs(a, 4); pxs(a, 5)
                if p is not None:
                    fin(p, 1)
                if a is not None:
                    pxs(a, 6); pxs(a, 7); hand(a)
            body(0, None)
            body(1, 0)
            with act.Fori(2, B) as i:
                body(i, i - 1)
            body(None, B - 1)

        @block.vector
        def _(dve):
            V = nc.vector
            V.memset(zeros[:, :], 0.0)
            V.memset(pw[:, 0:1], 1.0)
            V.memset(qc[:, :], 0.0).then_inc(s_pw, 1)
            dve.wait_ge(s_pw, 1)
            dve.wait_ge(s_lam, 2)
            V.tensor_tensor_scan(pw[:, 1:P + 1], lam[:, 1:2].to_broadcast([P, P]), zeros[:, :], 1.0, ALU.mult, ALU.add).then_inc(s_pw, 1)
            dve.wait_ge(s_pw, 2)
            V.tensor_copy(rp[:, :], pw[:, P::-1]).then_inc(s_tab, 1)
            dve.wait_ge(s_tab, 1)
            dve.wait_ge(s_init, 1)

            def stats(src, st, mv, bn, ag, b, g):
                for m in tiles(g):
                    last = V.bn_stats(st[:, m, :], src[:, m, :])
                last.then_inc(bn, 1)
                dve.wait_ge(bn, nth(b, 2, g + 1))
                V.memset(tick[:, :], 0.0)
                for m in tiles(g):
                    last = V.bn_aggr(mv[:, m, :], st[:, m, :])
                last.then_inc(ag, 1)
                dve.wait_ge(ag, nth(b, 2, g + 1))

            def twice_normed(vv, mv, g):
                s = slice(4 * g, 4 * g + 4)
                V.tensor_scalar(vv[:, s, 0], mv[:, s, 1], EPS, None, ALU.add)
                return V.tensor_scalar(vv[:, s, 1], mv[:, s, 1], 1.0 + EPS, EPS * EPS, ALU.mult, ALU.add)

            def ln1(a, g):
                dve.wait_ge(h_cp, nth(a, 2, g + 1))
                stats(h, st1, mv1, bn1, ag1, a, g)
                twice_normed(vv1, mv1, g).then_inc(var1, 1)

            def normed(a, g):
                dve.wait_ge(r1_ok, nth(a, 2, g + 1))
                for m in tiles(g):
                    last = V.tensor_scalar(nl[:, m, :], h[:, m, :], mv1[:, m, 0:1], rr1[:, m, 1:2], ALU.subtract, ALU.mult)
                last.then_inc(nl_ok, 1)

            def mixes(a):
                dve.wait_ge(hl_ok, nth(a, 2, 2))
                dve.wait_ge(d_ok, nth(a, 1, 1))
                for dst, n in ((xq, "tm_q"), (xk, "tm_k"), (xv, "tm_v"), (xg, "tm_g")):
                    V.scalar_tensor_tensor(dst[:, 0:T], d[:, 0:T], col(n), hl[:, 0:T], ALU.mult, ALU.add).then_inc(mix, 1)

            def tokens(a, i):
                dve.wait_ge(rq_ok, nth(a, 2, i + 1))
                V.tensor_scalar(nrm[:, i, :], nrm[:, i, :], P ** -0.5, 1e-8, ALU.mult, ALU.add).then_inc(nr_ok, 1)
                dve.wait_ge(nr_ok, nth(a, 2, i + 1))
                V.reciprocal(rin[:, i, :], nrm[:, i, :]).then_inc(ri_ok, 1)
                dve.wait_ge(ri_ok, nth(a, 2, i + 1))
                for m in range(TILES):
                    last = V.tensor_scalar(qk[i][:, m, :], qk[i][:, m, :], rin[:, i, m:m + 1], None, ALU.mult)
                last.then_inc(tok, 1)

            def qlev(a, g):
                dve.wait_ge(eq, nth(a, 2, g + 1))
                if g:
                    dve.wait_ge(qx_in, nth(a, 256, 128))
                else:
                    before(dve, qx_in, a, 256, 256)
                src, w = q[:, HALF * g:HALF * g + scan_w[g]], scan_w[g]
                for at, m, n in ((Q8, EIGHT, 0), (Q32, WIN, 0), (Q4, EIGHT, FOUR)):
                    view = lambda ap, m: ap.rearrange("p (x m) -> p x m", m=m)
                    dst = ql[:, at - HALF:at - HALF + w * (m - n) // m]
                    last = V.tensor_tensor(view(dst, m - n), view(src, m)[:, :, n:m], over(pw[:, 0:m - n], w // m, m - n), ALU.mult)
                last.then_inc(ql_ok, 1)

            def inter(a):
                dve.wait_ge(ek, nth(a, 2, 2))
                V.tensor_tensor(kc[:, :].rearrange("p (n m) -> p n m", n=NST),
                                k[:, 0:NST * P].rearrange("p (n m) -> p n m", n=NST), over(rp[:, 1:P + 1], NST, P), ALU.mult).then_inc(kc_ok, 1)
                V.tensor_tensor_scan(z[:, 0:T], lam[:, 1:2].to_broadcast([P, T]), k[:, 0:T], 0.0, ALU.mult, ALU.add).then_inc(z_ok, 1)
                V.tensor_tensor(qc[:, :].rearrange("p (n m) -> p n m", n=TILES),
                                q[:, :].rearrange("p (n m) -> p n m", n=TILES), over(pw[:, 1:P + 1], TILES, P), ALU.mult).then_inc(qc_ok, 1)
                dve.wait_ge(z_ok, nth(a, 1, 1))
                dve.wait_ge(front, used(a, "v1"))
                V.tensor_tensor(qz[:, 0:T], q[:, 0:T], z[:, 0:T], ALU.mult).then_inc(qz_ok, 1)

            def denominators(a, g):
                dve.wait_ge(front, used(a, f"z{g}"))
                V.reciprocal(gz[:, cols(g)], bf(f"z{g}")[:, 0:width[g]]).then_inc(rz_ok, 1)
                dve.wait_ge(rz_ok, nth(a, 2, g + 1))
                dve.wait_ge(th_ok, nth(a, 2, g + 1))
                V.scalar_tensor_tensor(gz[:, cols(g)], th[:, cols(g)], 1.0, gz[:, cols(g)], ALU.add, ALU.mult).then_inc(gz_ok, 1)

            def chain(a):
                for c in range(NST):
                    U = bf(f"u{c // 4}")[:, P * (c % 4):P * (c % 4) + P]
                    dve.wait_ge(front, used(a, f"u{c // 4}"))
                    if c == 0:
                        before(dve, ab_ok, a, 1, 1)
                        V.tensor_copy(af[:, 0, :], U).then_inc(af_ok, 1)
                    else:
                        dve.wait_ge(af_ok, nth(a, NST, c))
                        V.scalar_tensor_tensor(af[:, c, :], af[:, c - 1, :], pw[:, P:P + 1], U, ALU.mult, ALU.add).then_inc(af_ok, 1)

            def merge(a, c):
                D, rows = bank[c % 2], WIN * windows[c]
                dve.wait_ge(diag, nth(a, TILES, c + 1))
                if c >= 2:
                    dve.wait_ge(px_ok, nth(a, TILES, c - 1))
                else:
                    before(dve, px_ok, a, TILES, TILES - 1 + c)
                n = 2 * TILES
                heads = lambda ap, m: ap.rearrange("p (h m) -> p h m", h=HEADS)
                pdc = pd[c % 2][0:rows, :]
                V.tensor_copy(heads(pdc, WIN)[:, :, EIGHT:WIN], heads(D[0:rows, SW:2 * SW], WIN)[:, :, EIGHT:WIN]).then_inc(merged, 1)
                dve.wait_ge(merged, nth(a, n, 2 * c + 1))
                V.memset(tick[:, :], 0.0)
                V.copy_predicated(pdc, mask[0:rows, 0:SW], D[0:rows, 0:SW]).then_inc(merged, 1)
                dve.wait_ge(merged, nth(a, n, 2 * c + 2))
                V.memset(tick[:, :], 0.0)
                V.copy_predicated(pdc.rearrange("p (x m) -> p x m", m=EIGHT)[:, :, FOUR:EIGHT],
                                  mask[0:rows, SW:SW + SW // 2].rearrange("p (x m) -> p x m", m=FOUR),
                                  D[0:rows, 2 * SW:2 * SW + SW // 2].rearrange("p (x m) -> p x m", m=FOUR)).then_inc(pd_ok, 1)

            def gated(a, g):
                dve.wait_ge(s_out, nth(a, TILES, 4 * g + 4))
                dve.wait_ge(gz_ok, nth(a, 2, g + 1))
                before(dve, mlp, a, len(MLP), MLP.index(f"wo{g}") + 1)
                V.scalar_tensor_tensor(ga[:, cols(g)], bank[3][:, 0:width[g]], 0.5, gz[:, cols(g)], ALU.mult, ALU.mult).then_inc(ga_ok, 1)

            def hand(a):
                for m in range(TILES):
                    last = V.tensor_scalar(a_out[:, m, :], h[:, m, :], mv1[:, m, 0:1], rr1[:, m, 0:1], ALU.subtract, ALU.mult)
                last.then_inc(aa_ok, 1)

            def attended(p, g):
                dve.wait_ge(mlp, used_b(p, f"wo{g}"))
                dve.wait_ge(aa_ok, nth(p, 1, 1))
                s = slice(4 * g, 4 * g + 4)
                V.tensor_tensor(x2[:, s, :], bm(f"wo{g}")[:, :].rearrange("p (m n) -> p m n", m=4), a_out[:, s, :], ALU.add).then_inc(x2_ok, 1)
                dve.wait_ge(x2_ok, nth(p, 2, g + 1))
                stats(x2, st2, mv2, bn2, ag2, p, g)
                V.tensor_scalar(vv2[:, s], mv2[:, s, 1], EPS, None, ALU.add).then_inc(var2, 1)

            def normed2(p, g):
                dve.wait_ge(r2_ok, nth(p, 2, g + 1))
                for m in tiles(g):
                    last = V.tensor_scalar(nl2[:, m, :], x2[:, m, :], mv2[:, m, 0:1], rr2[:, m:m + 1], ALU.subtract, ALU.mult)
                last.then_inc(nl2_ok, 1)

            def hidden(p, g):
                dve.wait_ge(mlp, used_b(p, f"w2_{g}"))
                dve.wait_ge(t_ok, nth(p, 2, g + 1))
                s = slice(4 * g, 4 * g + 4)
                V.tensor_tensor(h1[:, s, :], bm(f"w2_{g}")[:, :].rearrange("p (m n) -> p m n", m=4), t[:, s, :], ALU.add).then_inc(h1_ok, 1)
                dve.wait_ge(h1_ok, nth(p, 2, g + 1))
                stats(h1, st3, mv3, bn3, ag3, p, g)
                twice_normed(vv3, mv3, g).then_inc(var3, 1)

            def normed3(p, g):
                dve.wait_ge(r3_ok, nth(p, 2, g + 1))
                dve.wait_ge(mlp, used_b(p, f"n2T{g}"))
                for m in tiles(g):
                    V.tensor_scalar(n1[:, m, :], h1[:, m, :], mv3[:, m, 0:1], rr3[:, m, 0:1], ALU.subtract, ALU.mult)
                    last = V.tensor_scalar(n2[:, m, :], h1[:, m, :], mv3[:, m, 0:1], rr3[:, m, 1:2], ALU.subtract, ALU.mult)
                last.then_inc(n12_ok, 1)

            def x_attn(p, g):
                dve.wait_ge(mlp, used_b(p, f"at{g}"))
                dve.wait_ge(n1T_ok, nth(p, 2, g + 1))
                V.scalar_tensor_tensor(xa[:, cols(g)], bm(f"at{g}")[:, 0:width[g]], col("at_b"), xa[:, cols(g)], ALU.add, ALU.add).then_inc(xa_ok, 1)

            def result(p, g):
                dve.wait_ge(mlp, used_b(p, f"oT{g}"))
                s = slice(4 * g, 4 * g + 4)
                V.tensor_tensor(h1[:, s, :], bm(f"oT{g}")[:, :].rearrange("p (m n) -> p m n", m=4), h1[:, s, :], ALU.add).then_inc(y_ok, 1)

            def body(a, p):
                if a is not None:
                    ln1(a, 0); ln1(a, 1)
                if p is not None:
                    attended(p, 0); attended(p, 1)
                if a is not None:
                    normed(a, 0); normed(a, 1)
                if p is not None:
                    normed2(p, 0); normed2(p, 1)
                if a is not None:
                    mixes(a); tokens(a, 0); tokens(a, 1)
                if p is not None:
                    hidden(p, 0); hidden(p, 1)
                if a is not None:
                    qlev(a, 0); inter(a)
                if p is not None:
                    normed3(p, 0); normed3(p, 1); x_attn(p, 0)
                if a is not None:
                    denominators(a, 0); denominators(a, 1); chain(a); hand(a)
                    merge(a, 0); merge(a, 1); merge(a, 2); merge(a, 3); qlev(a, 1)
                    gated(a, 0)
                if p is not None:
                    x_attn(p, 1); result(p, 0)
                if a is not None:
                    merge(a, 4); merge(a, 5)
                if p is not None:
                    result(p, 1)
                if a is not None:
                    merge(a, 6); merge(a, 7); gated(a, 1)
            body(0, None)
            body(1, 0)
            with dve.Fori(2, B) as i:
                body(i, i - 1)
            body(None, B - 1)

        @block.tensor
        def _(pe):
            mm = nc.tensor.matmul
            pe.wait_ge(s_w, 28 * 16)
            pe.wait_ge(s_fc2, 16)
            fc2 = hid[:, :, :].rearrange("p j (a n) -> p (j a) n", a=2)
            for e in range(E):
                for j in range(4):
                    last = mm(bank[e][:, P * j:P * j + P], fc2[:, e, P * j:P * j + P], wnext[:, :], start=True, stop=True)
                last.then_inc(s_gp, 1)
            pe.wait_ge(s_gc, 1)
            mm(bank[0][:, 0:E], wnext[:, :], fc2b[:, :], start=True, stop=True).then_inc(s_gp, 1)
            pe.wait_ge(s_gc, E + 1)
            pe.wait_ge(s_init, 1)

            def product(bk, src, w, g):
                for i, m in enumerate(tiles(g)):
                    last = mm(bk[:, P * i:P * i + P], src[:, P * m:P * m + P], w[:, :], start=True, stop=True)
                return last

            def transposed(bk, src, ms):
                for i, m in enumerate(ms):
                    last = nc.tensor.transpose(bk[:, P * i:P * i + P], src(m), ident[:, :])
                return last

            def dcts(a, g):
                bk = front_bank(pe, a, f"dct{g}")
                pe.wait_ge(x_in, nth(a, 32, 32))
                product(bk, xT, dct, g).then_inc(front, 1)

            def nTs(a, g):
                bk = front_bank(pe, a, f"nT{g}")
                pe.wait_ge(nl_ok, nth(a, 2, g + 1))
                transposed(bk, lambda m: nl[:, m, :], tiles(g)).then_inc(front, 1)

            def qkv(a, name, g):
                i = "qkv".index(name)
                bk = front_bank(pe, a, f"{name}{g}")
                pe.wait_ge(mix, nth(a, 4, i + 1))
                product(bk, (xq, xk, xv)[i], (wq, wk, wv)[i], g).then_inc(front, 1)

            def gates(a, g):
                bk = front_bank(pe, a, f"g{g}")
                pe.wait_ge(mix, nth(a, 4, 4))
                mm(bk[:, 0:width[g]], wg[:, :], xg[:, cols(g)], start=True, stop=True).then_inc(front, 1)

            def qkTs(a, i, g):
                bk = front_bank(pe, a, f"{'qk'[i]}T{g}")
                pe.wait_ge(tok, nth(a, 2, i + 1))
                transposed(bk, lambda m: qk[i][:, m, :], tiles(g)).then_inc(front, 1)

            def kcs(a, g):
                bk = front_bank(pe, a, f"kc{g}")
                pe.wait_ge(kc_ok, nth(a, 1, 1))
                transposed(bk, lambda m: kc[:, P * m:P * m + P], range(4 * g, min(4 * g + 4, NST))).then_inc(front, 1)

            def zs(a, g):
                bk = front_bank(pe, a, f"z{g}")
                pe.wait_ge(qz_ok, nth(a, 1, 1))
                mm(bk[:, 0:width[g]], heads1[:, :], qz[:, cols(g)], start=True, stop=True).then_inc(front, 1)

            def us(a, g):
                bk = front_bank(pe, a, f"u{g}")
                pe.wait_ge(kcT_ok, nth(a, 2, g + 1))
                pe.wait_ge(v_ok, nth(a, 2, g + 1))
                for i, c in enumerate(range(4 * g, min(4 * g + 4, NST))):
                    last = mm(bk[:, P * i:P * i + P], kcT[:, c, :], v[:, c, :], start=True, stop=True)
                last.then_inc(front, 1)

            def pairs(a, c):
                g, lc, n = c // 4, c % 4, windows[c]
                if c >= 2:
                    pe.wait_ge(pd_ok, nth(a, TILES, c - 1))
                else:
                    pe.wait_ge(af_ok, nth(a, NST, (4, NST)[c]))
                if lc == 0:
                    pe.wait_ge(qx_in, nth(a, 256, 128 * (g + 1)))
                    pe.wait_ge(kl_ok, nth(a, 2, g + 1))
                D, O = bank[c % 2], bank[2]
                for w in range(n):
                    r, wl = slice(WIN * w, WIN * w + WIN), 4 * lc + w
                    kr, score = slice(WIN * wl, WIN * wl + WIN), lambda at, m: D[r, at:at + HEADS * m].rearrange("p (h n) -> p h n", h=HEADS)
                    for j in range(FOUR):
                        lhs = k[:, HALF * g + WIN * wl:HALF * g + WIN * wl + WIN] if j == 0 else ki[:, j - 1, kr]
                        mm(score(0, WIN)[:, :, j:WIN:FOUR], lhs, qx[:, :, WIN * wl + j:WIN * wl + WIN:FOUR], start=True, stop=True)
                    for j in range(1, NE):
                        t0 = EIGHT * j
                        mm(score(SW, WIN)[:, :, t0:t0 + EIGHT], ko[:, j - 1, kr],
                           qx[:, :, Q8 + WIN * wl + t0:Q8 + WIN * wl + t0 + EIGHT], start=True, stop=True)
                    last = mm(score(2 * SW, WIN // 2), kh[:, kr], qx[:, :, Q4 + WIN // 2 * wl:Q4 + WIN // 2 * wl + WIN // 2],
                              start=True, stop=True)
                last.then_inc(diag, 1)
                if c >= 1:
                    pe.wait_ge(px_ok, nth(a, TILES, c))
                else:
                    pe.wait_ge(rz_ok, nth(a, 2, 1))
                for w in range(1, n):
                    rows = WIN * w if w < 3 else P
                    last = mm(O[0:rows, SW * (w - 1):SW * w].rearrange("p (h n) -> p h n", h=HEADS), kw[:, w - 1, P * lc:P * lc + rows],
                              qx[:, :, Q32 + P * lc + WIN * w:Q32 + P * lc + WIN * w + WIN], start=True, stop=True)
                last.then_inc(off, 1)

            def scan(a, c):
                n, s0 = WIN * windows[c], P * (c % 4)
                if c == 0:
                    pe.wait_ge(rz_ok, nth(a, 2, 2))
                    pe.wait_ge(v_ok, nth(a, 2, 2))
                if c == 4:
                    pe.wait_ge(ga_ok, nth(a, 2, 1))
                if c == 1:
                    pe.wait_ge(ab_ok, nth(a, 1, 1))
                    pe.wait_ge(qc_ok, nth(a, 1, 1))
                if c:
                    mm(bank[3][:, s0:s0 + n], ab[:, c - 1, :], qc[:, P * c:P * c + n], start=True, stop=False, skip_group_check=True)
                pe.wait_ge(px_ok, nth(a, TILES, c + 1))
                for hd in range(HEADS):
                    r = slice(HD * hd, HD * hd + HD)
                    last = mm(bank[3][r, s0:s0 + n], v[:, c, r], px[c % 2][:, hd, 0:n], start=(c == 0), stop=True, skip_group_check=True)
                last.then_inc(s_out, 1)

            def attends(p, g):
                bk = mlp_bank(pe, p, f"wo{g}")
                pe.wait_ge(ga_ok, nth(p, 2, g + 1))
                product(bk, ga, wo, g).then_inc(mlp, 1)

            def n2Ts(p, g):
                bk = mlp_bank(pe, p, f"n2T{g}")
                pe.wait_ge(nl2_ok, nth(p, 2, g + 1))
                transposed(bk, lambda m: nl2[:, m, :], tiles(g)).then_inc(mlp, 1)

            def w1s(p, g):
                pe.wait_ge(n2T_ok, nth(p, 2, g + 1))
                for j in range(4):
                    bk = mlp_bank(pe, p, f"w1_{g}{j}")
                    mm(bk[:, 0:width[g]], w1[:, P * j:P * j + P], c1[:, cols(g)], start=True, stop=True).then_inc(mlp, 1)

            def w2s(p, g):
                bk = mlp_bank(pe, p, f"w2_{g}")
                pe.wait_ge(ge1, nth(p, 8, 4 * g + 4))
                for i, m in enumerate(tiles(g)):
                    for j in range(4):
                        last = mm(bk[:, P * i:P * i + P], hid[:, j, P * m:P * m + P], w2[:, j, :], start=(j == 0), stop=(j == 3))
                last.then_inc(mlp, 1)

            def nTT(p, g):
                bk = mlp_bank(pe, p, f"n1T{g}")
                pe.wait_ge(n12_ok, nth(p, 2, g + 1))
                transposed(bk, lambda m: n1[:, m, :], tiles(g)).then_inc(mlp, 1)
                bk = mlp_bank(pe, p, f"nmT{g}")
                transposed(bk, lambda m: n2[:, m, :], tiles(g)).then_inc(mlp, 1)

            def ats(p, g):
                bk = mlp_bank(pe, p, f"at{g}")
                pe.wait_ge(nmT_ok, nth(p, 2, g + 1))
                mm(bk[:, 0:width[g]], wat[:, :], c1[:, cols(g)], start=True, stop=True).then_inc(mlp, 1)

            def f1s(p, g):
                pe.wait_ge(xa_ok, nth(p, 2, g + 1))
                pe.wait_ge(e_in, nth(p, 48, 48))
                for j in range(4):
                    bk = mlp_bank(pe, p, f"f1_{g}{j}")
                    mm(bk[:, 0:width[g]], f1w[:, P * j:P * j + P], xa[:, cols(g)], start=True, stop=True).then_inc(mlp, 1)

            def f2s(p, g):
                bk = mlp_bank(pe, p, f"f2_{g}")
                for j in range(4):
                    pe.wait_ge(ge2, nth(p, 8, 4 * g + j + 1))
                    last = mm(bk[:, 0:width[g]], f2w[:, P * j:P * j + P], hid[:, j, cols(g)], start=(j == 0), stop=(j == 3))
                last.then_inc(mlp, 1)

            def oTs(p, g):
                bk = mlp_bank(pe, p, f"oT{g}")
                pe.wait_ge(fin_ok, nth(p, 2, g + 1))
                transposed(bk, lambda m: c1[:, P * m:P * m + P], tiles(g)).then_inc(mlp, 1)

            def body(a, p):
                if a is not None:
                    dcts(a, 0); dcts(a, 1)
                if p is not None:
                    attends(p, 0); attends(p, 1)
                if a is not None:
                    nTs(a, 0); nTs(a, 1)
                if p is not None:
                    n2Ts(p, 0); w1s(p, 0)
                if a is not None:
                    for name in "qk":
                        qkv(a, name, 0); qkv(a, name, 1)
                if p is not None:
                    n2Ts(p, 1); w1s(p, 1)
                if a is not None:
                    qkv(a, "v", 0); qkv(a, "v", 1); gates(a, 0); gates(a, 1)
                if p is not None:
                    w2s(p, 0); w2s(p, 1)
                if a is not None:
                    qkTs(a, 0, 0); qkTs(a, 0, 1); qkTs(a, 1, 0); qkTs(a, 1, 1)
                if p is not None:
                    nTT(p, 0); ats(p, 0)
                if a is not None:
                    kcs(a, 0); kcs(a, 1); zs(a, 0); zs(a, 1); us(a, 0); us(a, 1)
                if p is not None:
                    f1s(p, 0)
                if a is not None:
                    pairs(a, 0); pairs(a, 1); scan(a, 0); pairs(a, 2); scan(a, 1); pairs(a, 3); scan(a, 2); scan(a, 3)
                if p is not None:
                    nTT(p, 1); ats(p, 1); f2s(p, 0); oTs(p, 0); f1s(p, 1)
                if a is not None:
                    pairs(a, 4); pairs(a, 5); scan(a, 4)
                if p is not None:
                    f2s(p, 1); oTs(p, 1)
                if a is not None:
                    pairs(a, 6); scan(a, 5); pairs(a, 7); scan(a, 6); scan(a, 7)
            body(0, None)
            body(1, 0)
            with pe.Fori(2, B) as i:
                body(i, i - 1)
            body(None, B - 1)


def kernel(**inputs):
    import numpy as np
    import concourse.bacc as bacc
    from concourse.bass_utils import run_bass_kernel_spmd

    I = {n: np.asarray(a) for n, a in inputs.items()}
    at = lambda n: I["L0_attn_" + n]
    ff = lambda n: I["L0_ffn_" + n]
    C = np.ascontiguousarray
    x = I["x"]
    full = x.shape[1] // P
    hd = np.arange(P) // HD
    arrays = {
        "xT": C(x[:, :full * P].reshape(x.shape[0], full, P).transpose(0, 2, 1)),
        "xtail": C(x[:, full * P:]),
        "ident": np.eye(P, dtype=np.float32),
        "heads1": (hd[:, None] == hd[None, :]).astype(np.float32),
        "dct": dct_basis(), "mask": pair_mask(),
        "wqT": C(at("Wq").T), "wkT": C(at("Wk").T), "wvT": C(at("Wv").T), "wgT": C(at("Wg").T),
        "woT": C(at("Wo").T), "w1T": C(at("W1").T), "w2T": C(at("W2").T),
        "watT": C(ff("attn_w").T), "wnextT": C(ff("next_w").T),
        "fc1T": C(ff("fc1_w").transpose(0, 2, 1)), "fc2": C(ff("fc2_w")),
        "fc1b": C(ff("fc1_b").reshape(-1, 4, P).transpose(0, 2, 1)), "fc2bT": C(ff("fc2_b").T),
        "ln1_g": at("ln1_g"), "ln1_b": at("ln1_b"), "ln2_g": at("ln2_g"), "ln2_b": at("ln2_b"),
        "td": at("time_decay"), "tm_q": at("tm_q").reshape(-1), "tm_k": at("tm_k").reshape(-1),
        "tm_v": at("tm_v").reshape(-1), "tm_g": at("tm_g").reshape(-1), "rms": at("rms_scale"),
        "f_g": ff("ln_g"), "f_b": ff("ln_b"), "at_b": ff("attn_b"), "nx_b": ff("next_b"),
    }
    arrays = {n: C(a) for n, a in arrays.items()}
    nc = bacc.Bacc("TRN2", target_bir_lowering=False, num_devices=1)
    aps = {n: nc.dram_tensor(f"in_{n}", a.shape, mybir.dt.from_np(a.dtype), kind="ExternalInput").ap()
           for n, a in arrays.items()}
    out = nc.dram_tensor("out_0", (x.shape[0], full + 1, P), F32, kind="ExternalOutput").ap()
    program(nc, aps, out)
    r = run_bass_kernel_spmd(nc, [{f"in_{n}": a for n, a in arrays.items()}], core_ids=[0])
    return r.results[0]["out_0"]
```

```python
import concourse.bass as bass
from concourse import mybir
from contextlib import ExitStack

F32 = mybir.dt.float32
U32 = mybir.dt.uint32
ALU = mybir.AluOpType
ACT = mybir.ActivationFunctionType

P = 128
HEADS = 4
HD = P // HEADS
WIN = 32
HALF = 512
EPS = 1e-5
EIGHT, FOUR = 8, 4
NW, NE = P // WIN, WIN // EIGHT
GRP = 2 * P
Q8, Q32, Q4 = GRP, 2 * GRP, 3 * GRP
QCOLS = 3 * GRP + GRP // 2
SW = HEADS * WIN

DIAG, BETWEEN, SOUT, FRONT0, REST0 = 0, 1, 2, 3, 5
FRONT = ["dct0", "dct1", "nT0", "nT1", "q0", "q1", "k0", "k1", "v0", "v1", "qT0", "qT1", "kT0", "kT1",
         "g0", "g1", "kc0", "kc1", "u", "zt", "rT0", "rT1"]
REST = (["wo0", "wo1", "n2T0", "n2T1"] + [f"w1_0{j}" for j in range(4)] + [f"w1_1{j}" for j in range(4)]
        + ["w2_0", "w2_1", "n1T0", "nmT0", "n1T1", "nmT1", "at0", "at1"] + [f"f1_0{j}" for j in range(4)]
        + ["f2_0"] + [f"f1_1{j}" for j in range(4)] + ["oT0", "f2_1", "oT1"])


def pair_mask():
    import numpy as np
    s = np.arange(P)[:, None] % WIN
    t = np.arange(WIN)[None, :]
    half = t[:, t[0] % EIGHT >= FOUR]
    cols = [(s // FOUR == t // FOUR) & (s <= t)] * HEADS
    cols += [(s // EIGHT == half // EIGHT) & (s % EIGHT < FOUR)] * HEADS
    return np.concatenate(cols, axis=1).astype(np.uint32)


def dct_basis():
    import numpy as np
    k = np.arange(P)[:, None].astype(np.float64)
    t = np.arange(P)[None, :].astype(np.float64)
    scale = np.full((P, 1), np.sqrt(2.0 / P))
    scale[0, 0] = np.sqrt(1.0 / P)
    return np.ascontiguousarray((scale * np.cos(np.pi * (2.0 * t + 1.0) * k / (2.0 * P))).astype(np.float32).T)


def program(nc, A, out):
    B, _, full = A["xT"].shape
    T = full + 1
    TAIL = A["xtail"].shape[1]
    E = A["fc1T"].shape[0]
    TILES = -(-T // P)
    PADT = TILES * P
    WINS = -(-T // WIN)
    last_rows = T - (TILES - 1) * P
    width = [HALF, T - HALF]
    GROUPS = TILES // 2
    scan_w = [min(GRP, WINS * WIN - GRP * j) for j in range(GROUPS)]
    windows = [min(4, WINS - 4 * c) for c in range(TILES)]
    NST = TILES - 1

    ctx = ExitStack()
    with ctx:
        def sb(name, *shape, dt=F32):
            return ctx.enter_context(nc.sbuf_tensor(name, [P, *shape], dt))

        def sem(name):
            return ctx.enter_context(nc.semaphore(name))

        ident, heads1, dct = sb("ident", P), sb("heads1", P), sb("dct", P)
        mask = sb("mask", SW + SW // 2, dt=U32)
        wq, wk, wv, wg, wo, wat, wnext = (sb(n, P) for n in ("wq", "wk", "wv", "wg", "wo", "wat", "wnext"))
        bq, bk_, bv, bg = (sb(n, P) for n in ("bq", "bk", "bv", "bg"))
        untm = sb("untm", 4)
        dec = sb("dec", HD, NST)
        w1 = sb("w1", 4 * P)
        w2 = sb("w2", 4, P)
        vec = sb("vec", 16)
        VEC = {n: i for i, n in enumerate(
            ["ln1_g", "ln1_b", "ln2_g", "ln2_b", "td", "tm_q", "tm_k", "tm_v", "tm_g", "rms", "f_g", "f_b",
             "at_b", "nx_b"])}
        col = lambda n: vec[:, VEC[n]:VEC[n] + 1]
        fc2b = sb("fc2b", E)
        lam = sb("lam", 2)
        pw = sb("pw", P + 1)
        rp = sb("rp", P + 1)
        zeros = sb("zeros", P)
        tick = sb("tick", 1)
        nhalf = sb("nhalf", 8)
        phalf = sb("phalf", 8)
        f1w = sb("f1w", 4 * P)
        f2w = sb("f2w", 4 * P + 1)
        f1b = sb("f1b", 4)
        g_dram = nc.dram_tensor("g_dram", [E, P, 4 * P + 1], F32, kind="Internal").ap()

        SH = TILES * P
        def h_parts(name):
            hs = sb(name, SH + 4 * TILES)
            return (hs, hs[:, 0:SH].rearrange("p (m n) -> p m n", m=TILES),
                    hs[:, SH:SH + 2 * TILES].rearrange("p (m n) -> p m n", m=TILES),
                    hs[:, SH + 2 * TILES:].rearrange("p (m n) -> p m n", m=TILES))
        hs0, h, mv1, rr1 = h_parts("hs0")
        hs1 = h_parts("hs1")[0]
        hs2, h_m, mv_m, rr_m = h_parts("hs2")
        xT = sb("xT", PADT)
        nl = sb("nl", TILES, P)
        st1, vv1 = sb("st1", TILES, 6), sb("vv1", TILES, 2)
        hl = sb("hl", PADT + 1)
        qk = [sb("qtok", TILES, P), sb("ktok", TILES, P)]
        squared = [nl, sb("squared", TILES, P)]
        ssq, nrm, rin = sb("ssq", 2, TILES), sb("nrm", 2, TILES), sb("rin", 2, TILES)
        v_f, gate_f = sb("v_f", TILES, P), sb("gate_f", PADT)
        q, k = sb("q", PADT), sb("k", PADT)
        zq = sb("zq", PADT)
        rz = sb("rz", TILES * HEADS)
        kc, kcT = sb("kc", NST * P), sb("kcT", NST, P)
        af = sb("af", HD * NST)

        v, gz = sb("v", TILES, P), sb("gz", PADT)
        ql = sb("ql", QCOLS - GRP)
        qx = sb("qx", 2, HEADS, QCOLS)
        ki, kh, ko, kw = (sb("ki", FOUR, 2 * GRP), sb("kh", 2 * GRP), sb("ko", NE - 1, 2 * GRP), sb("kw", NW - 1, 2 * GRP))
        qc = sb("qc", PADT)
        ab = sb("ab", NST, P)
        pd = [sb(f"pd{i}", HEADS * WIN) for i in range(2)]
        px = [sb(f"px{i}", HEADS, P) for i in range(2)]
        ga = sb("ga", PADT)

        x2, nl2, t_sum = sb("x2", TILES, P), sb("nl2", TILES, P), sb("t_sum", TILES, P)
        st2, mv2, vv2, rr2 = sb("st2", TILES, 6), sb("mv2", TILES, 2), sb("vv2", TILES), sb("rr2", TILES)
        st3, mv3, vv3, rr3 = sb("st3", TILES, 6), sb("mv3", TILES, 2), sb("vv3", TILES, 2), sb("rr3", TILES, 2)
        h1, n1, n2 = t_sum, nl2, x2
        c1, xa = sb("c1", PADT), sb("xa", PADT)
        hid = sb("hid", 4, PADT)

        bank = [ctx.enter_context(nc.psum_tensor(f"bank{i}", [P, 512], F32)) for i in range(8)]

        s_w = sem("s_w"); s_fc2 = sem("s_fc2"); s_zero = sem("s_zero"); s_init = sem("s_init")
        s_gp = sem("s_gp"); s_gc = sem("s_gc"); s_gd = sem("s_gd"); s_lam = sem("s_lam"); s_pw = sem("s_pw")
        s_tab = sem("s_tab")
        s_mix = sem("s_mix"); s_dec = sem("s_dec")
        x_in = sem("x_in")
        e_in = sem("e_in")
        qx_in = sem("qx_in")
        v_in = sem("v_in"); gz_in = sem("gz_in"); hs1_in = sem("hs1_in"); hs2_in = sem("hs2_in")
        o_out = sem("o_out")
        front = sem("front")
        rest = sem("rest")
        diag = sem("diag")
        off = sem("off")
        s_out = sem("s_out")
        h_cp = sem("h_cp"); hl_ok = sem("hl_ok")
        raw = sem("raw")
        v_ok = sem("v_ok"); th_ok = sem("th_ok"); eq = sem("eq"); ek = sem("ek"); kcT_ok = sem("kcT_ok")
        px_ok = sem("px_ok")
        n2T_ok = sem("n2T_ok"); n1T_ok = sem("n1T_ok"); nmT_ok = sem("nmT_ok"); fin_ok = sem("fin_ok")
        ge1 = sem("ge1"); ge2 = sem("ge2")
        bn1 = sem("bn1"); ag1 = sem("ag1"); var1 = sem("var1"); nl_ok = sem("nl_ok")
        nr_ok = sem("nr_ok"); ri_ok = sem("ri_ok"); tok = sem("tok")
        ql_ok = sem("ql_ok")
        kc_ok = sem("kc_ok"); z_ok = sem("z_ok"); qz_ok = sem("qz_ok"); rz_ok = sem("rz_ok")
        af_ok = sem("af_ok"); qc_ok = sem("qc_ok")
        gate_ok = sem("gate_ok"); ga_ok = sem("ga_ok")
        pd_ok = sem("pd_ok"); merged = sem("merged")
        aa_ok = sem("aa_ok")
        x2_ok = sem("x2_ok"); bn2 = sem("bn2"); ag2 = sem("ag2"); var2 = sem("var2"); nl2_ok = sem("nl2_ok")
        h1_ok = sem("h1_ok"); bn3 = sem("bn3"); ag3 = sem("ag3"); var3 = sem("var3"); n12_ok = sem("n12_ok")
        xa_ok = sem("xa_ok"); y_ok = sem("y_ok")
        r1_ok = sem("r1_ok"); rq_ok = sem("rq_ok"); r2_ok = sem("r2_ok"); r3_ok = sem("r3_ok"); t_ok = sem("t_ok")
        ab_ok = sem("ab_ok")
        kl_ok = sem("kl_ok")

        def nth(b, per, n):
            return b * per + n

        def first(b):
            return isinstance(b, int) and b == 0

        def before(eng, s, b, per, n):
            if not first(b):
                eng.wait_ge(s, (b - 1) * per + n)

        emptied = {"zt": (rz_ok, 1, 1), "u": (af_ok, 1, 1)}
        for g in (0, 1):
            for name, s in (("dct", h_cp), ("nT", hl_ok), ("v", v_ok), ("g", th_ok), ("qT", eq), ("kT", ek),
                            ("kc", kcT_ok), ("rT", gate_ok), ("wo", x2_ok), ("n2T", n2T_ok), ("w2_", h1_ok),
                            ("n1T", n1T_ok), ("nmT", nmT_ok), ("at", xa_ok), ("f2_", fin_ok), ("oT", y_ok)):
                emptied[f"{name}{g}"] = (s, 2, g + 1)
            emptied[f"q{g}"] = (raw, 4, g + 1)
            emptied[f"k{g}"] = (raw, 4, g + 3)
            for j in range(4):
                emptied[f"w1_{g}{j}"] = (ge1, 8, 4 * g + j + 1)
                emptied[f"f1_{g}{j}"] = (ge2, 8, 4 * g + j + 1)

        def free_bank(pe, b, order, banks, name):
            n = order.index(name)
            if n >= banks:
                s, per, i = emptied[order[n - banks]]
                pe.wait_ge(s, nth(b, per, i))
            else:
                last = max(j for j in range(len(order)) if j % banks == n)
                s, per, i = emptied[order[last]]
                before(pe, s, b, per, i)

        def bf(name):
            return bank[FRONT0 + FRONT.index(name) % 2]

        def bm(name):
            return bank[REST0 + REST.index(name) % 3]

        def front_bank(pe, b, name):
            free_bank(pe, b, FRONT, 2, name)
            return bf(name)

        def rest_bank(pe, b, name):
            free_bank(pe, b, REST, 3, name)
            return bm(name)

        def used(b, name):
            return nth(b, len(FRONT), FRONT.index(name) + 1)

        def used_m(b, name):
            return nth(b, len(REST), REST.index(name) + 1)

        def last_use(eng, b, g):
            if g >= 2:
                eng.wait_ge(off, nth(b, TILES, 2 * g - 2))
            else:
                before(eng, off, b, TILES, 2 * g + 6)

        def rounds(eng, body):
            def at(n):
                return [n - d if 0 <= n - d < B else None for d in range(4)]
            for n in range(3):
                body(*at(n))
            with eng.Fori(3, B) as i:
                body(i, i - 1, i - 2, i - 3)
            for n in range(B, B + 3):
                body(*at(n))

        def cols(g):
            return slice(HALF * g, HALF * g + width[g])

        def tiles(g):
            return range(4 * g, 4 * g + 4)

        def over(ap, n, m):
            return ap.rearrange("p (o m) -> p o m", o=1).to_broadcast([P, n, m])

        block = ctx.enter_context(nc.Block())

        @block.sync
        def _(sp):
            G = qx[:, :, :, :].rearrange("p g h n -> p (g h n)")[:, 0:E * (4 * P + 1)].rearrange("p (e n) -> p e n", e=E)
            loads = [(ident, A["ident"]), (heads1, A["heads1"]), (dct, A["dct"]), (mask, A["mask"]),
                     (wq, A["wqT"]), (wk, A["wkT"]), (wv, A["wvT"]), (wg, A["wgT"]), (wo, A["woT"]),
                     (wat, A["watT"]), (wnext, A["wnextT"]), (w1, A["w1T"]), (fc2b, A["fc2bT"])]
            sp.dma_start(hid[:, :, :].rearrange("p j (a n) -> p (j a) n", a=2), A["fc2"].rearrange("e d n -> d e n")).then_inc(s_fc2, 16)
            for dst, src in loads:
                sp.dma_start(dst[:, :], src).then_inc(s_w, 16)
            sp.dma_start(w2[:, :, :], A["w2T"].rearrange("(j p) n -> p j n", p=P)).then_inc(s_w, 16)
            for name, i in VEC.items():
                sp.dma_start(vec[:, i:i + 1], A[name].rearrange("(p o) -> p o", o=1)).then_inc(s_w, 16)

            def samples(b, at):
                if not first(b):
                    sp.wait_ge(front, used(b - 1, "dct1"))
                sp.dma_start(xT[:, 0:full], A["xT"][at, :, :]).then_inc(x_in, 16)
                sp.dma_start(xT[0:TAIL, full:T], A["xtail"][at, :].rearrange("(p o) -> p o", o=1)).then_inc(x_in, 16)

            sp.wait_ge(s_zero, 1)
            samples(0, 0)
            sp.wait_ge(s_gc, E + 1)
            sp.dma_start(g_dram.rearrange("e p n -> p e n"), G).then_inc(s_gd, 16)
            sp.wait_ge(s_gd, 16)
            sp.wait_ge(s_init, 1)

            def expert(m):
                e = m % E
                before(sp, fin_ok, m, 2, 2)
                sp.dma_start(f1w[:, :], A["fc1T"][e, :, :]).then_inc(e_in, 16)
                sp.dma_start(f1b[:, :], A["fc1b"][e, :, :]).then_inc(e_in, 16)
                sp.dma_start(f2w[:, :], g_dram[e, :, :]).then_inc(e_in, 16)

            def spread(b, g):
                sp.wait_ge(ql_ok, nth(b, GROUPS, g + 1))
                for hd in range(HEADS):
                    rows = slice(HD * hd, HD * hd + HD)
                    sp.dma_start(qx[rows, g % 2, hd, 0:scan_w[g]], q[rows, GRP * g:GRP * g + scan_w[g]]).then_inc(qx_in, 16)
                    sp.dma_start(qx[rows, g % 2, hd, GRP:QCOLS], ql[rows, :]).then_inc(qx_in, 16)

            def hand_v(s):
                before(sp, s_out, s, TILES, TILES)
                sp.dma_start(v[:, :, :], v_f[:, :, :]).then_inc(v_in, 16)

            def hand_gate(s):
                sp.wait_ge(gate_ok, nth(s, 2, 2))
                sp.dma_start(gz[:, :], gate_f[:, :]).then_inc(gz_in, 16)

            def hand_h(f, s, m):
                if s is not None:
                    if m is not None:
                        sp.wait_ge(t_ok, nth(m, 2, 2))
                    sp.dma_start(hs2[:, :], hs1[:, :]).then_inc(hs2_in, 16)
                if f is not None:
                    if s is not None:
                        handed, there = nth(s, 16, 16), nth(f, 2, 2)
                        sp.wait_ge(hs2_in, handed)
                        sp.wait_ge(nl_ok, there)
                    else:
                        sp.wait_ge(nl_ok, nth(f, 2, 2))
                    sp.dma_start(hs1[:, :], hs0[:, :]).then_inc(hs1_in, 16)

            def store(p, g):
                sp.wait_ge(y_ok, nth(p, 2, g + 1))
                r0 = HALF * g
                whole = 4 - g
                sp.dma_start(out[p, r0:r0 + whole * P, :].rearrange("(m p) n -> p m n", p=P),
                             h1[:, 4 * g:4 * g + whole, :]).then_inc(o_out, 16)
                if g:
                    sp.dma_start(out[p, (TILES - 1) * P:T, :], h1[0:last_rows, TILES - 1, :]).then_inc(o_out, 16)

            def body(f, s, m, t):
                if s is not None:
                    hand_v(s); spread(s, 1); hand_gate(s)
                if m is not None:
                    expert(m)
                if f is not None:
                    samples(f + 1, (f + 1) % B)
                if t is not None:
                    store(t, 1)
                if s is not None:
                    spread(s, 2)
                if f is not None or s is not None:
                    hand_h(f, s, m)
                if s is not None:
                    spread(s, 3)
                if f is not None:
                    spread(f, 0)
                if m is not None:
                    store(m, 0)
            rounds(sp, body)
            sp.wait_ge(o_out, 48 * B)

        @block.gpsimd
        def _(gp):
            gp.memset(xT[:, :], 0.0).then_inc(s_zero, 1)
            for tile in (nhalf, phalf):
                gp.memset(tile[:, :], -0.5 if tile is nhalf else 0.5)
            gp.memset(zq[:, :], 1.0)
            for tile in (q, k, qc, ga, hl, kh, ql, gate_f, pd[0], pd[1]):
                gp.memset(tile[:, :], 0.0)
            for tile in (ki, ko, kw, px[0], px[1]):
                gp.memset(tile[:, :, :], 0.0)
            gp.memset(c1[:, :], 0.0)
            gp.memset(xa[:, :], 0.0)
            gp.wait_ge(s_fc2, 16)
            gp.wait_ge(s_gc, E)
            gp.memset(hid[:, :, :], 0.0)
            gp.wait_ge(s_gd, 16)
            gp.memset(qx[:, :, :, :], 0.0).then_inc(s_init, 1)
            gp.wait_ge(s_tab, 1)

            def pow1(a, g):
                gp.wait_ge(var1, nth(a, 2, g + 1))
                gp.tensor_tensor(rr1[:, 4 * g:4 * g + 4, :], vv1[:, 4 * g:4 * g + 4, :],
                                 nhalf[:, 0:8].rearrange("p (m o) -> p m o", o=2), ALU.pow).then_inc(r1_ok, 1)

            def powq(a, i):
                gp.wait_ge(raw, nth(a, 4, 2 * i + 2))
                gp.tensor_tensor(nrm[:, i, :], ssq[:, i, :], phalf[:, 0:TILES], ALU.pow).then_inc(rq_ok, 1)

            def klev(b, g):
                gp.wait_ge(ek, nth(b, 2, g // 2 + 1))
                last_use(gp, b, g)
                parts = [(ki[:, 0, :], FOUR, 1, 0)]
                parts += [(ki[:, j, :], FOUR, j + 1, j) for j in range(1, FOUR)]
                parts += [(kh[:, :], EIGHT, FOUR, FOUR)]
                parts += [(ko[:, j - 1, :], WIN, EIGHT * j, EIGHT * j) for j in range(1, NE)]
                parts += [(kw[:, w - 1, :], P, WIN * w, WIN * w) for w in range(1, NW)]
                for dst, m, n, ref in parts:
                    w = GRP if m == P else scan_w[g]
                    view = lambda ap: ap.rearrange("p (x m) -> p x m", m=m)[:, :, 0:n]
                    last = gp.tensor_tensor(view(dst[:, GRP * (g % 2):GRP * (g % 2) + w]), view(k[:, GRP * g:GRP * g + w]),
                                            over(rp[:, P - ref:P - ref + n], w // m, n), ALU.mult)
                last.then_inc(kl_ok, 1)

            def states(b):
                gp.wait_ge(af_ok, nth(b, 1, 1))
                before(gp, s_out, b, TILES, TILES)
                wide = [P, NST, HEADS, HD]
                gp.tensor_tensor(ab[:, :, :].rearrange("p c (h e) -> p c h e", h=HEADS),
                                 af[:, :].rearrange("p (o e c) -> p c o e", o=1, e=HD).to_broadcast(wide),
                                 heads1[:, :].rearrange("p (o h e) -> p o h e", o=1, h=HEADS).to_broadcast(wide), ALU.mult).then_inc(ab_ok, 1)

            def pow2(p, g):
                gp.wait_ge(var2, nth(p, 2, g + 1))
                gp.tensor_tensor(rr2[:, 4 * g:4 * g + 4], vv2[:, 4 * g:4 * g + 4], nhalf[:, 0:4], ALU.pow).then_inc(r2_ok, 1)

            def resid(p, g):
                before(gp, o_out, p, 48, 48)
                gp.wait_ge(x2_ok, nth(p, 2, g + 1))
                gp.tensor_tensor(t_sum[:, 4 * g:4 * g + 4, :], x2[:, 4 * g:4 * g + 4, :], h_m[:, 4 * g:4 * g + 4, :],
                                 ALU.add).then_inc(t_ok, 1)

            def pow3(p, g):
                gp.wait_ge(var3, nth(p, 2, g + 1))
                gp.tensor_tensor(rr3[:, 4 * g:4 * g + 4, :], vv3[:, 4 * g:4 * g + 4, :],
                                 nhalf[:, 0:8].rearrange("p (m o) -> p m o", o=2), ALU.pow).then_inc(r3_ok, 1)

            def body(f, s, m, t):
                if s is not None:
                    states(s); klev(s, 1)
                if f is not None:
                    pow1(f, 0); pow1(f, 1)
                if m is not None:
                    pow2(m, 0); pow2(m, 1)
                if s is not None:
                    klev(s, 2)
                if m is not None:
                    resid(m, 0); resid(m, 1)
                if f is not None:
                    powq(f, 0); powq(f, 1)
                if m is not None:
                    pow3(m, 0)
                if s is not None:
                    klev(s, 3)
                if m is not None:
                    pow3(m, 1)
                if f is not None:
                    klev(f, 0)
            rounds(gp, body)

        @block.scalar
        def _(act):
            G = qx[:, :, :, :].rearrange("p g h n -> p (g h n)")[:, 0:E * (4 * P + 1)].rearrange("p (e n) -> p e n", e=E)
            for e in range(E):
                act.wait_ge(s_gp, e + 1)
                nc.scalar.activation(G[:, e, 0:4 * P], bank[e][:, :], ACT.Copy).then_inc(s_gc, 1)
            act.wait_ge(s_gp, E + 1)
            nc.scalar.activation(G[:, :, 4 * P], bank[0][:, 0:E], ACT.Identity, bias=col("nx_b")).then_inc(s_gc, 1)
            act.wait_ge(s_w, 28 * 16)
            nc.scalar.activation(lam[:, 0:1], col("td"), ACT.Exp).then_inc(s_lam, 1)
            act.wait_ge(s_lam, 1)
            nc.scalar.activation(lam[:, 1:2], lam[:, 0:1], ACT.Exp, scale=-1.0).then_inc(s_lam, 1)

            def hcopy(a, g):
                act.wait_ge(front, used(a, f"dct{g}"))
                before(act, hs1_in, a, 16, 16)
                nc.scalar.activation(h[:, 4 * g:4 * g + 4, :], bf(f"dct{g}")[:, :].rearrange("p (m n) -> p m n", m=4), ACT.Copy).then_inc(h_cp, 1)

            def hlT(a, g):
                act.wait_ge(front, used(a, f"nT{g}"))
                nc.scalar.activation(hl[:, 1 + HALF * g:1 + HALF * g + width[g]], bf(f"nT{g}")[:, 0:width[g]], ACT.Identity,
                                     scale=col("ln1_g"), bias=col("ln1_b")).then_inc(hl_ok, 1)

            def squares(a, i, g):
                name = f"{'qk'[i]}{g}"
                act.wait_ge(front, used(a, name))
                nc.scalar.activation(qk[i][:, 4 * g:4 * g + 4, :], bf(name)[:, :].rearrange("p (m n) -> p m n", m=4), ACT.Copy)
                for m in range(4):
                    last = nc.scalar.activation(squared[i][:, 4 * g + m, :], bf(name)[:, P * m:P * m + P], ACT.Square,
                                                accum_out=ssq[:, i, 4 * g + m:4 * g + m + 1])
                last.then_inc(raw, 1)

            def vcopy(a, g):
                act.wait_ge(front, used(a, f"v{g}"))
                before(act, v_in, a, 16, 16)
                nc.scalar.activation(v_f[:, 4 * g:4 * g + 4, :], bf(f"v{g}")[:, :].rearrange("p (m n) -> p m n", m=4), ACT.Copy).then_inc(v_ok, 1)

            def gate(a, g):
                act.wait_ge(front, used(a, f"g{g}"))
                before(act, gz_in, a, 16, 16)
                nc.scalar.activation(gate_f[:, cols(g)], bf(f"g{g}")[:, 0:width[g]], ACT.Tanh, scale=0.5).then_inc(th_ok, 1)

            def exps(a, i, g):
                name = f"{'qk'[i]}T{g}"
                act.wait_ge(front, used(a, name))
                if i == 0:
                    before(act, qx_in, a, 512, 512)
                    before(act, qc_ok, a, 1, 1)
                else:
                    before(act, kl_ok, a, GROUPS, GROUPS)
                nc.scalar.activation((q, k)[i][:, cols(g)], bf(name)[:, 0:width[g]], ACT.Exp,
                                     scale=col("rms")).then_inc((eq, ek)[i], 1)

            def kcopy(a, g):
                n = (4, NST - 4)[g]
                act.wait_ge(front, used(a, f"kc{g}"))
                nc.scalar.activation(kcT[:, 4 * g:4 * g + n, :], bf(f"kc{g}")[:, 0:P * n].rearrange("p (m n) -> p m n", m=n), ACT.Copy).then_inc(kcT_ok, 1)

            def pxs(a, c):
                X, O, n = px[c % 2], bank[BETWEEN], windows[c]
                if c >= 2:
                    act.wait_ge(s_out, nth(a, TILES, c - 1))
                else:
                    before(act, s_out, a, TILES, TILES - 1 + c)
                act.wait_ge(off, nth(a, TILES, c + 1))
                for w in range(1, n):
                    nc.scalar.activation(X[0:WIN * w, :, WIN * w:WIN * w + WIN],
                                         O[0:WIN * w, SW * (w - 1):SW * w].rearrange("p (h n) -> p h n", h=HEADS), ACT.Copy)
                act.wait_ge(pd_ok, nth(a, TILES, c + 1))
                for w in range(n):
                    r = slice(WIN * w, WIN * w + WIN)
                    last = nc.scalar.activation(X[r, :, r], pd[c % 2][r, :].rearrange("p (h n) -> p h n", h=HEADS), ACT.Copy)
                last.then_inc(px_ok, 1)

            def n2T(p, g):
                act.wait_ge(rest, used_m(p, f"n2T{g}"))
                nc.scalar.activation(c1[:, cols(g)], bm(f"n2T{g}")[:, 0:width[g]], ACT.Identity,
                                     scale=col("ln2_g"), bias=col("ln2_b")).then_inc(n2T_ok, 1)

            def gelu1(p, g):
                for j in range(4):
                    act.wait_ge(rest, used_m(p, f"w1_{g}{j}"))
                    nc.scalar.activation(hid[:, j, cols(g)], bm(f"w1_{g}{j}")[:, 0:width[g]], ACT.Gelu).then_inc(ge1, 1)

            def nT(p, g):
                act.wait_ge(rest, used_m(p, f"n1T{g}"))
                nc.scalar.activation(xa[:, cols(g)], bm(f"n1T{g}")[:, 0:width[g]], ACT.Copy).then_inc(n1T_ok, 1)
                act.wait_ge(rest, used_m(p, f"nmT{g}"))
                nc.scalar.activation(c1[:, cols(g)], bm(f"nmT{g}")[:, 0:width[g]], ACT.Identity,
                                     scale=col("f_g"), bias=col("f_b")).then_inc(nmT_ok, 1)

            def gelu2(p, g):
                act.wait_ge(e_in, nth(p, 48, 48))
                for j in range(4):
                    act.wait_ge(rest, used_m(p, f"f1_{g}{j}"))
                    nc.scalar.activation(hid[:, j, cols(g)], bm(f"f1_{g}{j}")[:, 0:width[g]], ACT.Gelu,
                                         bias=f1b[:, j:j + 1]).then_inc(ge2, 1)

            def fin(p, g):
                act.wait_ge(rest, used_m(p, f"f2_{g}"))
                nc.scalar.activation(c1[:, cols(g)], bm(f"f2_{g}")[:, 0:width[g]], ACT.Gelu,
                                     bias=f2w[:, 4 * P:4 * P + 1]).then_inc(fin_ok, 1)

            def body(f, s, m, t):
                if s is not None:
                    pxs(s, 0)
                if f is not None:
                    hcopy(f, 0); hcopy(f, 1)
                if t is not None:
                    fin(t, 1)
                if s is not None:
                    pxs(s, 1)
                if f is not None:
                    hlT(f, 0); hlT(f, 1)
                if m is not None:
                    n2T(m, 0); n2T(m, 1)
                if s is not None:
                    pxs(s, 2)
                if f is not None:
                    squares(f, 0, 0); squares(f, 0, 1)
                if m is not None:
                    gelu1(m, 0)
                if f is not None:
                    squares(f, 1, 0); squares(f, 1, 1)
                if s is not None:
                    pxs(s, 3)
                if m is not None:
                    gelu1(m, 1)
                if f is not None:
                    vcopy(f, 0); vcopy(f, 1)
                if s is not None:
                    pxs(s, 4); pxs(s, 5)
                if f is not None:
                    for i in (0, 1):
                        exps(f, i, 0); exps(f, i, 1)
                    gate(f, 0); gate(f, 1)
                if m is not None:
                    nT(m, 0)
                if s is not None:
                    pxs(s, 6)
                if m is not None:
                    nT(m, 1)
                if f is not None:
                    kcopy(f, 0); kcopy(f, 1)
                if m is not None:
                    gelu2(m, 0)
                if s is not None:
                    pxs(s, 7)
                if m is not None:
                    fin(m, 0); gelu2(m, 1)
            rounds(act, body)

        @block.vector
        def _(dve):
            V = nc.vector
            V.memset(zeros[:, :], 0.0)
            V.memset(pw[:, 0:1], 1.0)
            V.memset(dec[:, :, :], 0.0).then_inc(s_pw, 1)
            dve.wait_ge(s_pw, 1)
            dve.wait_ge(s_lam, 2)
            V.tensor_tensor_scan(pw[:, 1:P + 1], lam[:, 1:2].to_broadcast([P, P]), zeros[:, :], 1.0, ALU.mult, ALU.add).then_inc(s_pw, 1)
            dve.wait_ge(s_pw, 2)
            V.tensor_copy(dec[:, :, 1:NST], over(pw[:, P:P + 1], HD, 1).to_broadcast([P, HD, NST - 1])).then_inc(s_dec, 1)
            V.tensor_copy(rp[:, :], pw[:, P::-1]).then_inc(s_tab, 1)
            for i, n in enumerate(("tm_q", "tm_k", "tm_v", "tm_g")):
                last = V.tensor_scalar(untm[:, i:i + 1], col(n), -1.0, 1.0, ALU.mult, ALU.add)
            last.then_inc(s_mix, 1)
            dve.wait_ge(s_mix, 1)
            for i, (w, prev) in enumerate(((wq, bq), (wk, bk_), (wv, bv), (wg, bg))):
                last = V.tensor_scalar(prev[:, :], w[:, :], untm[:, i:i + 1], None, ALU.mult)
            last.then_inc(s_mix, 1)
            dve.wait_ge(s_mix, 2)
            for w, n in ((wq, "tm_q"), (wk, "tm_k"), (wv, "tm_v"), (wg, "tm_g")):
                last = V.tensor_scalar(w[:, :], w[:, :], col(n), None, ALU.mult)
            last.then_inc(s_mix, 1)
            dve.wait_ge(s_mix, 3)
            dve.wait_ge(s_tab, 1)
            dve.wait_ge(s_dec, 1)
            dve.wait_ge(s_init, 1)

            def stats(src, st, mv, bn, ag, b, g):
                for m in tiles(g):
                    last = V.bn_stats(st[:, m, :], src[:, m, :])
                last.then_inc(bn, 1)
                dve.wait_ge(bn, nth(b, 2, g + 1))
                V.memset(tick[:, :], 0.0)
                for m in tiles(g):
                    last = V.bn_aggr(mv[:, m, :], st[:, m, :])
                last.then_inc(ag, 1)
                dve.wait_ge(ag, nth(b, 2, g + 1))

            def twice_normed(vv, mv, g):
                s = slice(4 * g, 4 * g + 4)
                V.tensor_scalar(vv[:, s, 0], mv[:, s, 1], EPS, None, ALU.add)
                return V.tensor_scalar(vv[:, s, 1], mv[:, s, 1], 1.0 + EPS, EPS * EPS, ALU.mult, ALU.add)

            def ln1(a, g):
                dve.wait_ge(h_cp, nth(a, 2, g + 1))
                stats(h, st1, mv1, bn1, ag1, a, g)
                twice_normed(vv1, mv1, g).then_inc(var1, 1)

            def normed(a, g):
                dve.wait_ge(r1_ok, nth(a, 2, g + 1))
                for m in tiles(g):
                    last = V.tensor_scalar(nl[:, m, :], h[:, m, :], mv1[:, m, 0:1], rr1[:, m, 1:2], ALU.subtract, ALU.mult)
                last.then_inc(nl_ok, 1)

            def tokens(a, i):
                dve.wait_ge(rq_ok, nth(a, 2, i + 1))
                V.tensor_scalar(nrm[:, i, :], nrm[:, i, :], P ** -0.5, 1e-8, ALU.mult, ALU.add).then_inc(nr_ok, 1)
                dve.wait_ge(nr_ok, nth(a, 2, i + 1))
                V.reciprocal(rin[:, i, :], nrm[:, i, :]).then_inc(ri_ok, 1)
                dve.wait_ge(ri_ok, nth(a, 2, i + 1))
                for m in range(TILES):
                    last = V.tensor_scalar(qk[i][:, m, :], qk[i][:, m, :], rin[:, i, m:m + 1], None, ALU.mult)
                last.then_inc(tok, 1)

            def qlev(b, g):
                dve.wait_ge(eq, nth(b, 2, g // 2 + 1))
                last_use(dve, b, g)
                if g:
                    dve.wait_ge(qx_in, nth(b, 512, 128 * g))
                else:
                    before(dve, qx_in, b, 512, 512)
                src, w = q[:, GRP * g:GRP * g + scan_w[g]], scan_w[g]
                for at, m, n in ((Q8, EIGHT, 0), (Q32, WIN, 0), (Q4, EIGHT, FOUR)):
                    view = lambda ap, m: ap.rearrange("p (x m) -> p x m", m=m)
                    dst = ql[:, at - GRP:at - GRP + w * (m - n) // m]
                    last = V.tensor_tensor(view(dst, m - n), view(src, m)[:, :, n:m], over(pw[:, 0:m - n], w // m, m - n), ALU.mult)
                last.then_inc(ql_ok, 1)

            def inter(f):
                dve.wait_ge(ek, nth(f, 2, 2))
                V.tensor_tensor(kc[:, :].rearrange("p (n m) -> p n m", n=NST),
                                k[:, 0:NST * P].rearrange("p (n m) -> p n m", n=NST), over(rp[:, 1:P + 1], NST, P), ALU.mult).then_inc(kc_ok, 1)
                V.tensor_tensor_scan(zq[:, 0:T], lam[:, 1:2].to_broadcast([P, T]), k[:, 0:T], 0.0, ALU.mult, ALU.add).then_inc(z_ok, 1)
                dve.wait_ge(z_ok, nth(f, 1, 1))
                V.tensor_tensor(zq[:, 0:T], q[:, 0:T], zq[:, 0:T], ALU.mult).then_inc(qz_ok, 1)

            def from_start(s):
                before(dve, s_out, s, TILES, TILES)
                V.tensor_tensor(qc[:, :].rearrange("p (n m) -> p n m", n=TILES),
                                q[:, :].rearrange("p (n m) -> p n m", n=TILES), over(pw[:, 1:P + 1], TILES, P), ALU.mult).then_inc(qc_ok, 1)

            def denominators(f):
                dve.wait_ge(front, used(f, "zt"))
                V.reciprocal(rz[:, :], bf("zt")[:, 0:TILES * HEADS]).then_inc(rz_ok, 1)

            def gates(s, g):
                dve.wait_ge(front, used(s, f"rT{g}"))
                V.scalar_tensor_tensor(gate_f[:, cols(g)], gate_f[:, cols(g)], 1.0, bf(f"rT{g}")[:, 0:width[g]], ALU.add, ALU.mult).then_inc(gate_ok, 1)

            def chain(f):
                dve.wait_ge(front, used(f, "u"))
                before(dve, ab_ok, f, 1, 1)
                V.tensor_tensor_scan(af[:, :], dec[:, :, :].rearrange("p e c -> p (e c)"), bf("u")[:, 0:HD * NST],
                                     0.0, ALU.mult, ALU.add).then_inc(af_ok, 1)

            def merge(a, c):
                D, rows = bank[DIAG], WIN * windows[c]
                dve.wait_ge(diag, nth(a, TILES, c + 1))
                if c >= 2:
                    dve.wait_ge(px_ok, nth(a, TILES, c - 1))
                else:
                    before(dve, px_ok, a, TILES, TILES - 1 + c)
                n = 2 * TILES
                heads = lambda ap, m: ap.rearrange("p (h m) -> p h m", h=HEADS)
                pdc = pd[c % 2][0:rows, :]
                V.tensor_copy(heads(pdc, WIN)[:, :, EIGHT:WIN], heads(D[0:rows, SW:2 * SW], WIN)[:, :, EIGHT:WIN]).then_inc(merged, 1)
                dve.wait_ge(merged, nth(a, n, 2 * c + 1))
                V.memset(tick[:, :], 0.0)
                V.copy_predicated(pdc, mask[0:rows, 0:SW], D[0:rows, 0:SW]).then_inc(merged, 1)
                dve.wait_ge(merged, nth(a, n, 2 * c + 2))
                V.memset(tick[:, :], 0.0)
                V.copy_predicated(pdc.rearrange("p (x m) -> p x m", m=EIGHT)[:, :, FOUR:EIGHT],
                                  mask[0:rows, SW:SW + SW // 2].rearrange("p (x m) -> p x m", m=FOUR),
                                  D[0:rows, 2 * SW:2 * SW + SW // 2].rearrange("p (x m) -> p x m", m=FOUR)).then_inc(pd_ok, 1)

            def gated(a, g):
                dve.wait_ge(s_out, nth(a, TILES, 4 * g + 4))
                dve.wait_ge(gz_in, nth(a, 16, 16))
                before(dve, rest, a, len(REST), REST.index(f"wo{g}") + 1)
                V.scalar_tensor_tensor(ga[:, cols(g)], bank[SOUT][:, 0:width[g]], 0.5, gz[:, cols(g)], ALU.mult, ALU.mult).then_inc(ga_ok, 1)

            def attn_in(m):
                dve.wait_ge(hs2_in, nth(m, 16, 16))
                for i in range(TILES):
                    last = V.tensor_scalar(x2[:, i, :], h_m[:, i, :], mv_m[:, i, 0:1], rr_m[:, i, 0:1], ALU.subtract, ALU.mult)
                last.then_inc(aa_ok, 1)

            def attended(p, g):
                dve.wait_ge(rest, used_m(p, f"wo{g}"))
                dve.wait_ge(aa_ok, nth(p, 1, 1))
                s = slice(4 * g, 4 * g + 4)
                V.tensor_tensor(x2[:, s, :], bm(f"wo{g}")[:, :].rearrange("p (m n) -> p m n", m=4), x2[:, s, :], ALU.add).then_inc(x2_ok, 1)
                dve.wait_ge(x2_ok, nth(p, 2, g + 1))
                stats(x2, st2, mv2, bn2, ag2, p, g)
                V.tensor_scalar(vv2[:, s], mv2[:, s, 1], EPS, None, ALU.add).then_inc(var2, 1)

            def normed2(p, g):
                dve.wait_ge(r2_ok, nth(p, 2, g + 1))
                for m in tiles(g):
                    last = V.tensor_scalar(nl2[:, m, :], x2[:, m, :], mv2[:, m, 0:1], rr2[:, m:m + 1], ALU.subtract, ALU.mult)
                last.then_inc(nl2_ok, 1)

            def hidden(p, g):
                dve.wait_ge(rest, used_m(p, f"w2_{g}"))
                dve.wait_ge(t_ok, nth(p, 2, g + 1))
                s = slice(4 * g, 4 * g + 4)
                V.tensor_tensor(h1[:, s, :], bm(f"w2_{g}")[:, :].rearrange("p (m n) -> p m n", m=4), t_sum[:, s, :], ALU.add).then_inc(h1_ok, 1)
                dve.wait_ge(h1_ok, nth(p, 2, g + 1))
                stats(h1, st3, mv3, bn3, ag3, p, g)
                twice_normed(vv3, mv3, g).then_inc(var3, 1)

            def normed3(p, g):
                dve.wait_ge(r3_ok, nth(p, 2, g + 1))
                dve.wait_ge(rest, used_m(p, f"n2T{g}"))
                for m in tiles(g):
                    V.tensor_scalar(n1[:, m, :], h1[:, m, :], mv3[:, m, 0:1], rr3[:, m, 0:1], ALU.subtract, ALU.mult)
                    last = V.tensor_scalar(n2[:, m, :], h1[:, m, :], mv3[:, m, 0:1], rr3[:, m, 1:2], ALU.subtract, ALU.mult)
                last.then_inc(n12_ok, 1)

            def x_attn(p, g):
                dve.wait_ge(rest, used_m(p, f"at{g}"))
                dve.wait_ge(n1T_ok, nth(p, 2, g + 1))
                V.scalar_tensor_tensor(xa[:, cols(g)], bm(f"at{g}")[:, 0:width[g]], col("at_b"), xa[:, cols(g)], ALU.add, ALU.add).then_inc(xa_ok, 1)

            def result(p, g):
                dve.wait_ge(rest, used_m(p, f"oT{g}"))
                s = slice(4 * g, 4 * g + 4)
                V.tensor_tensor(h1[:, s, :], bm(f"oT{g}")[:, :].rearrange("p (m n) -> p m n", m=4), h1[:, s, :], ALU.add).then_inc(y_ok, 1)

            def body(f, s, m, t):
                if s is not None:
                    merge(s, 0); from_start(s); qlev(s, 1); gates(s, 0); gates(s, 1)
                if f is not None:
                    ln1(f, 0); ln1(f, 1)
                if t is not None:
                    result(t, 1)
                if m is not None:
                    attn_in(m); attended(m, 0); attended(m, 1)
                if s is not None:
                    merge(s, 1)
                if f is not None:
                    normed(f, 0); normed(f, 1)
                if m is not None:
                    normed2(m, 0); normed2(m, 1)
                if s is not None:
                    merge(s, 2); qlev(s, 2); merge(s, 3)
                if f is not None:
                    tokens(f, 0)
                if m is not None:
                    hidden(m, 0)
                if f is not None:
                    tokens(f, 1)
                if s is not None:
                    merge(s, 4); gated(s, 0); qlev(s, 3)
                if m is not None:
                    hidden(m, 1)
                if s is not None:
                    merge(s, 5)
                if m is not None:
                    normed3(m, 0); normed3(m, 1)
                if s is not None:
                    merge(s, 6)
                if f is not None:
                    inter(f); qlev(f, 0)
                if m is not None:
                    x_attn(m, 0); x_attn(m, 1)
                if s is not None:
                    merge(s, 7)
                if f is not None:
                    chain(f); denominators(f)
                if m is not None:
                    result(m, 0)
                if s is not None:
                    gated(s, 1)
            rounds(dve, body)

        @block.tensor
        def _(pe):
            mm = nc.tensor.matmul
            pe.wait_ge(s_w, 28 * 16)
            pe.wait_ge(s_fc2, 16)
            fc2 = hid[:, :, :].rearrange("p j (a n) -> p (j a) n", a=2)
            for e in range(E):
                for j in range(4):
                    last = mm(bank[e][:, P * j:P * j + P], fc2[:, e, P * j:P * j + P], wnext[:, :], start=True, stop=True)
                last.then_inc(s_gp, 1)
            pe.wait_ge(s_gc, 1)
            mm(bank[0][:, 0:E], wnext[:, :], fc2b[:, :], start=True, stop=True).then_inc(s_gp, 1)
            pe.wait_ge(s_gc, E + 1)
            pe.wait_ge(s_init, 1)
            pe.wait_ge(s_mix, 3)

            def product(bk, src, w, g):
                for i, m in enumerate(tiles(g)):
                    last = mm(bk[:, P * i:P * i + P], src[:, P * m:P * m + P], w[:, :], start=True, stop=True)
                return last

            def transposed(bk, src, ms):
                for i, m in enumerate(ms):
                    last = nc.tensor.transpose(bk[:, P * i:P * i + P], src(m), ident[:, :])
                return last

            def dcts(a, g):
                bk = front_bank(pe, a, f"dct{g}")
                pe.wait_ge(x_in, nth(a, 32, 32))
                product(bk, xT, dct, g).then_inc(front, 1)

            def nTs(a, g):
                bk = front_bank(pe, a, f"nT{g}")
                pe.wait_ge(nl_ok, nth(a, 2, g + 1))
                transposed(bk, lambda m: nl[:, m, :], tiles(g)).then_inc(front, 1)

            def qkv(a, name, g):
                i = "qkv".index(name)
                bk = front_bank(pe, a, f"{name}{g}")
                pe.wait_ge(hl_ok, nth(a, 2, g + 1))
                for j, m in enumerate(tiles(g)):
                    mm(bk[:, P * j:P * j + P], hl[:, 1 + P * m:1 + P * m + P], (wq, wk, wv)[i][:, :], start=True, stop=False)
                    last = mm(bk[:, P * j:P * j + P], hl[:, P * m:P * m + P], (bq, bk_, bv)[i][:, :], start=False, stop=True)
                last.then_inc(front, 1)

            def gates(a, g):
                bk = front_bank(pe, a, f"g{g}")
                mm(bk[:, 0:width[g]], wg[:, :], hl[:, 1 + HALF * g:1 + HALF * g + width[g]], start=True, stop=False)
                mm(bk[:, 0:width[g]], bg[:, :], hl[:, cols(g)], start=False, stop=True).then_inc(front, 1)

            def qkTs(a, i, g):
                bk = front_bank(pe, a, f"{'qk'[i]}T{g}")
                pe.wait_ge(tok, nth(a, 2, i + 1))
                transposed(bk, lambda m: qk[i][:, m, :], tiles(g)).then_inc(front, 1)

            def kcs(a, g):
                bk = front_bank(pe, a, f"kc{g}")
                pe.wait_ge(kc_ok, nth(a, 1, 1))
                transposed(bk, lambda m: kc[:, P * m:P * m + P], range(4 * g, min(4 * g + 4, NST))).then_inc(front, 1)

            def zts(a):
                bk = front_bank(pe, a, "zt")
                pe.wait_ge(qz_ok, nth(a, 1, 1))
                for m in range(TILES):
                    last = mm(bk[:, HEADS * m:HEADS * m + HEADS], zq[:, P * m:P * m + P], heads1[:, 0:P:HD], start=True, stop=True)
                last.then_inc(front, 1)

            def rTs(a, g):
                bk = front_bank(pe, a, f"rT{g}")
                pe.wait_ge(rz_ok, nth(a, 1, 1))
                for i, m in enumerate(tiles(g)):
                    for hd in range(HEADS):
                        c = HEADS * m + hd
                        last = mm(bk[HD * hd:HD * hd + HD, P * i:P * i + P], rz[:, c:c + 1].to_broadcast([P, HD]), ident[:, :],
                                  start=True, stop=True)
                last.then_inc(front, 1)

            def us(f):
                bk = front_bank(pe, f, "u")
                pe.wait_ge(kcT_ok, nth(f, 2, 2))
                pe.wait_ge(v_ok, nth(f, 2, 2))
                for c in range(NST):
                    for hd in range(HEADS):
                        r = slice(HD * hd, HD * hd + HD)
                        last = mm(bk[r, c:HD * NST:NST], kcT[:, c, r], v_f[:, c, r], start=True, stop=True)
                last.then_inc(front, 1)

            def pairs(b, c):
                g, n, x = c // 2, windows[c], qx[:, c // 2 % 2, :, :]
                D, O = bank[DIAG], bank[BETWEEN]
                if c:
                    pe.wait_ge(pd_ok, nth(b, TILES, c))
                else:
                    before(pe, pd_ok, b, TILES, TILES)
                if c % 2 == 0:
                    pe.wait_ge(qx_in, nth(b, 512, 128 * (g + 1)))
                    pe.wait_ge(kl_ok, nth(b, GROUPS, g + 1))
                by_head = lambda ap: ap.rearrange("p (h n) -> p h n", h=HEADS)
                k0, q0 = GRP * (g % 2) + P * (c % 2), P * (c % 2)
                for w in range(n):
                    r, kr, t0 = slice(WIN * w, WIN * w + WIN), slice(k0 + WIN * w, k0 + WIN * w + WIN), q0 + WIN * w
                    for j in range(FOUR):
                        mm(by_head(D[r, 0:SW])[:, :, j:WIN:FOUR], ki[:, j, kr], x[:, :, t0 + j:t0 + WIN:FOUR], start=True, stop=True)
                    for j in range(1, NE):
                        mm(by_head(D[r, SW:2 * SW])[:, :, EIGHT * j:EIGHT * j + EIGHT], ko[:, j - 1, kr],
                           x[:, :, Q8 + t0 + EIGHT * j:Q8 + t0 + EIGHT * j + EIGHT], start=True, stop=True)
                    last = mm(by_head(D[r, 2 * SW:2 * SW + SW // 2]), kh[:, kr], x[:, :, Q4 + t0 // 2:Q4 + t0 // 2 + WIN // 2],
                              start=True, stop=True)
                last.then_inc(diag, 1)
                if c:
                    pe.wait_ge(px_ok, nth(b, TILES, c))
                else:
                    before(pe, px_ok, b, TILES, TILES)
                for w in range(1, n):
                    rows = WIN * w if w < 3 else P
                    last = mm(by_head(O[0:rows, SW * (w - 1):SW * w]), kw[:, w - 1, k0:k0 + rows],
                              x[:, :, Q32 + q0 + WIN * w:Q32 + q0 + WIN * w + WIN], start=True, stop=True)
                last.then_inc(off, 1)

            def scan(b, c):
                n, s0, S = WIN * windows[c], P * (c % 4), bank[SOUT]
                if c == 0:
                    before(pe, ga_ok, b, 2, 2)
                    pe.wait_ge(v_in, nth(b, 16, 16))
                if c == 4:
                    pe.wait_ge(ga_ok, nth(b, 2, 1))
                if c == 1:
                    pe.wait_ge(ab_ok, nth(b, 1, 1))
                    pe.wait_ge(qc_ok, nth(b, 1, 1))
                if c:
                    mm(S[:, s0:s0 + n], ab[:, c - 1, :], qc[:, P * c:P * c + n], start=True, stop=False, skip_group_check=True)
                pe.wait_ge(px_ok, nth(b, TILES, c + 1))
                for hd in range(HEADS):
                    r = slice(HD * hd, HD * hd + HD)
                    last = mm(S[r, s0:s0 + n], v[:, c, r], px[c % 2][:, hd, 0:n], start=(c == 0), stop=True, skip_group_check=True)
                last.then_inc(s_out, 1)

            def attends(p, g):
                bk = rest_bank(pe, p, f"wo{g}")
                pe.wait_ge(ga_ok, nth(p, 2, g + 1))
                product(bk, ga, wo, g).then_inc(rest, 1)

            def n2Ts(p, g):
                bk = rest_bank(pe, p, f"n2T{g}")
                pe.wait_ge(nl2_ok, nth(p, 2, g + 1))
                transposed(bk, lambda m: nl2[:, m, :], tiles(g)).then_inc(rest, 1)

            def w1s(p, g):
                pe.wait_ge(n2T_ok, nth(p, 2, g + 1))
                for j in range(4):
                    bk = rest_bank(pe, p, f"w1_{g}{j}")
                    mm(bk[:, 0:width[g]], w1[:, P * j:P * j + P], c1[:, cols(g)], start=True, stop=True).then_inc(rest, 1)

            def w2s(p, g):
                bk = rest_bank(pe, p, f"w2_{g}")
                pe.wait_ge(ge1, nth(p, 8, 4 * g + 4))
                for i, m in enumerate(tiles(g)):
                    for j in range(4):
                        last = mm(bk[:, P * i:P * i + P], hid[:, j, P * m:P * m + P], w2[:, j, :], start=(j == 0), stop=(j == 3))
                last.then_inc(rest, 1)

            def nTT(p, g):
                bk = rest_bank(pe, p, f"n1T{g}")
                pe.wait_ge(n12_ok, nth(p, 2, g + 1))
                transposed(bk, lambda m: n1[:, m, :], tiles(g)).then_inc(rest, 1)
                bk = rest_bank(pe, p, f"nmT{g}")
                transposed(bk, lambda m: n2[:, m, :], tiles(g)).then_inc(rest, 1)

            def ats(p, g):
                bk = rest_bank(pe, p, f"at{g}")
                pe.wait_ge(nmT_ok, nth(p, 2, g + 1))
                mm(bk[:, 0:width[g]], wat[:, :], c1[:, cols(g)], start=True, stop=True).then_inc(rest, 1)

            def f1s(p, g):
                pe.wait_ge(xa_ok, nth(p, 2, g + 1))
                pe.wait_ge(e_in, nth(p, 48, 48))
                for j in range(4):
                    bk = rest_bank(pe, p, f"f1_{g}{j}")
                    mm(bk[:, 0:width[g]], f1w[:, P * j:P * j + P], xa[:, cols(g)], start=True, stop=True).then_inc(rest, 1)

            def f2s(p, g):
                bk = rest_bank(pe, p, f"f2_{g}")
                for j in range(4):
                    pe.wait_ge(ge2, nth(p, 8, 4 * g + j + 1))
                    last = mm(bk[:, 0:width[g]], f2w[:, P * j:P * j + P], hid[:, j, cols(g)], start=(j == 0), stop=(j == 3))
                last.then_inc(rest, 1)

            def oTs(p, g):
                bk = rest_bank(pe, p, f"oT{g}")
                pe.wait_ge(fin_ok, nth(p, 2, g + 1))
                transposed(bk, lambda m: c1[:, P * m:P * m + P], tiles(g)).then_inc(rest, 1)

            def body(f, s, m, t):
                if s is not None:
                    pairs(s, 0)
                if t is not None:
                    f2s(t, 1)
                if s is not None:
                    rTs(s, 0); rTs(s, 1)
                if f is not None:
                    dcts(f, 0); dcts(f, 1)
                if t is not None:
                    oTs(t, 1)
                if m is not None:
                    attends(m, 0); attends(m, 1)
                if s is not None:
                    pairs(s, 1); scan(s, 0)
                if f is not None:
                    nTs(f, 0); nTs(f, 1)
                if m is not None:
                    n2Ts(m, 0); n2Ts(m, 1)
                if s is not None:
                    pairs(s, 2); scan(s, 1)
                if f is not None:
                    qkv(f, "q", 0); qkv(f, "q", 1)
                if m is not None:
                    w1s(m, 0)
                if f is not None:
                    qkv(f, "k", 0); qkv(f, "k", 1)
                if s is not None:
                    pairs(s, 3); scan(s, 2)
                if m is not None:
                    w1s(m, 1)
                if f is not None:
                    qkv(f, "v", 0); qkv(f, "v", 1)
                if m is not None:
                    w2s(m, 0)
                if s is not None:
                    pairs(s, 4); scan(s, 3)
                if m is not None:
                    w2s(m, 1)
                if f is not None:
                    qkTs(f, 0, 0); qkTs(f, 0, 1)
                if s is not None:
                    pairs(s, 5); scan(s, 4)
                if f is not None:
                    qkTs(f, 1, 0); qkTs(f, 1, 1); gates(f, 0); gates(f, 1)
                if m is not None:
                    nTT(m, 0)
                if s is not None:
                    pairs(s, 6); scan(s, 5)
                if m is not None:
                    nTT(m, 1); ats(m, 0); ats(m, 1)
                if f is not None:
                    kcs(f, 0); kcs(f, 1)
                if m is not None:
                    f1s(m, 0)
                if s is not None:
                    pairs(s, 7); scan(s, 6)
                if f is not None:
                    us(f)
                if m is not None:
                    f2s(m, 0); f1s(m, 1)
                if f is not None:
                    zts(f)
                if m is not None:
                    oTs(m, 0)
                if s is not None:
                    scan(s, 7)
            rounds(pe, body)


def kernel(**inputs):
    import numpy as np
    import concourse.bacc as bacc
    from concourse.bass_utils import run_bass_kernel_spmd

    I = {n: np.asarray(a) for n, a in inputs.items()}
    at = lambda n: I["L0_attn_" + n]
    ff = lambda n: I["L0_ffn_" + n]
    C = np.ascontiguousarray
    x = I["x"]
    full = x.shape[1] // P
    hd = np.arange(P) // HD
    arrays = {
        "xT": C(x[:, :full * P].reshape(x.shape[0], full, P).transpose(0, 2, 1)),
        "xtail": C(x[:, full * P:]),
        "ident": np.eye(P, dtype=np.float32),
        "heads1": (hd[:, None] == hd[None, :]).astype(np.float32),
        "dct": dct_basis(), "mask": pair_mask(),
        "wqT": C(at("Wq").T), "wkT": C(at("Wk").T), "wvT": C(at("Wv").T), "wgT": C(at("Wg").T),
        "woT": C(at("Wo").T), "w1T": C(at("W1").T), "w2T": C(at("W2").T),
        "watT": C(ff("attn_w").T), "wnextT": C(ff("next_w").T),
        "fc1T": C(ff("fc1_w").transpose(0, 2, 1)), "fc2": C(ff("fc2_w")),
        "fc1b": C(ff("fc1_b").reshape(-1, 4, P).transpose(0, 2, 1)), "fc2bT": C(ff("fc2_b").T),
        "ln1_g": at("ln1_g"), "ln1_b": at("ln1_b"), "ln2_g": at("ln2_g"), "ln2_b": at("ln2_b"),
        "td": at("time_decay"), "tm_q": at("tm_q").reshape(-1), "tm_k": at("tm_k").reshape(-1),
        "tm_v": at("tm_v").reshape(-1), "tm_g": at("tm_g").reshape(-1), "rms": at("rms_scale"),
        "f_g": ff("ln_g"), "f_b": ff("ln_b"), "at_b": ff("attn_b"), "nx_b": ff("next_b"),
    }
    arrays = {n: C(a) for n, a in arrays.items()}
    nc = bacc.Bacc("TRN2", target_bir_lowering=False, num_devices=1)
    aps = {n: nc.dram_tensor(f"in_{n}", a.shape, mybir.dt.from_np(a.dtype), kind="ExternalInput").ap()
           for n, a in arrays.items()}
    out = nc.dram_tensor("out_0", (x.shape[0], full + 1, P), F32, kind="ExternalOutput").ap()
    program(nc, aps, out)
    r = run_bass_kernel_spmd(nc, [{f"in_{n}": a for n, a in arrays.items()}], core_ids=[0])
    return r.results[0]["out_0"]
```

```python
import concourse.bass as bass
from concourse import mybir
from contextlib import ExitStack

F32 = mybir.dt.float32
U32 = mybir.dt.uint32
ALU = mybir.AluOpType
ACT = mybir.ActivationFunctionType

P = 128
HEADS = 4
HD = P // HEADS
WIN = 32
HALF = 512
EPS = 1e-5
EIGHT, FOUR = 8, 4
NW, NE = P // WIN, WIN // EIGHT
GRP = 2 * P
Q8, Q32, Q4 = GRP, 2 * GRP, 3 * GRP
QCOLS = 3 * GRP + GRP // 2
SW = HEADS * WIN

DIAG, BETWEEN, SOUT, FRONT0, REST0 = 0, 1, 2, 3, 5
FRONT = ["dct0", "dct1", "nT0", "nT1", "q0", "q1", "k0", "k1", "v0", "v1", "qT0", "qT1", "kT0", "kT1",
         "g0", "g1", "kc0", "kc1", "u", "zt", "rT0", "rT1"]
REST = (["wo0", "wo1", "n2T0", "n2T1"] + [f"w1_0{j}" for j in range(4)] + [f"w1_1{j}" for j in range(4)]
        + ["w2_0", "w2_1", "n1T0", "nmT0", "n1T1", "nmT1", "at0", "at1"] + [f"f1_0{j}" for j in range(4)]
        + ["f2_0", "oT0"] + [f"f1_1{j}" for j in range(4)] + ["f2_1", "oT1"])


def pair_mask():
    import numpy as np
    s = np.arange(P)[:, None] % WIN
    t = np.arange(WIN)[None, :]
    half = t[:, t[0] % EIGHT >= FOUR]
    cols = [(s // FOUR == t // FOUR) & (s <= t)] * HEADS
    cols += [(s // EIGHT == half // EIGHT) & (s % EIGHT < FOUR)] * HEADS
    return np.concatenate(cols, axis=1).astype(np.uint32)


def dct_basis():
    import numpy as np
    k = np.arange(P)[:, None].astype(np.float64)
    t = np.arange(P)[None, :].astype(np.float64)
    scale = np.full((P, 1), np.sqrt(2.0 / P))
    scale[0, 0] = np.sqrt(1.0 / P)
    return np.ascontiguousarray((scale * np.cos(np.pi * (2.0 * t + 1.0) * k / (2.0 * P))).astype(np.float32).T)


def program(nc, A, out):
    B, _, full = A["xT"].shape
    T = full + 1
    TAIL = A["xtail"].shape[1]
    E = A["fc1T"].shape[0]
    TILES = -(-T // P)
    PADT = TILES * P
    WINS = -(-T // WIN)
    last_rows = T - (TILES - 1) * P
    width = [HALF, T - HALF]
    GROUPS = TILES // 2
    scan_w = [min(GRP, WINS * WIN - GRP * j) for j in range(GROUPS)]
    windows = [min(4, WINS - 4 * c) for c in range(TILES)]
    NST = TILES - 1

    ctx = ExitStack()
    with ctx:
        def sb(name, *shape, dt=F32):
            return ctx.enter_context(nc.sbuf_tensor(name, [P, *shape], dt))

        def sem(name):
            return ctx.enter_context(nc.semaphore(name))

        ident, heads1, dct = sb("ident", P), sb("heads1", P), sb("dct", P)
        mask = sb("mask", SW + SW // 2, dt=U32)
        wq, wk, wv, wg, wo, wat, wnext = (sb(n, P) for n in ("wq", "wk", "wv", "wg", "wo", "wat", "wnext"))
        dec = sb("dec", HD, NST)
        w1 = sb("w1", 4 * P)
        w2 = sb("w2", 4, P)
        vec = sb("vec", 14)
        VEC = {n: i for i, n in enumerate(
            ["ln1_g", "ln1_b", "ln2_g", "ln2_b", "td", "tm_q", "tm_k", "tm_v", "tm_g", "rms", "f_g", "f_b",
             "at_b", "nx_b"])}
        col = lambda n: vec[:, VEC[n]:VEC[n] + 1]
        fc2b = sb("fc2b", E)
        lam = sb("lam", 2)
        pw = sb("pw", P + 1)
        rp = sb("rp", P + 1)
        zeros = sb("zeros", P)
        tick = sb("tick", 1)
        nhalf = sb("nhalf", 8)
        phalf = sb("phalf", 8)
        f1w = sb("f1w", 4 * P)
        f2w = sb("f2w", 4 * P + 1)
        f1b = sb("f1b", 4)
        g_dram = nc.dram_tensor("g_dram", [E, P, 4 * P + 1], F32, kind="Internal").ap()

        SH = TILES * P
        def h_parts(name):
            hs = sb(name, SH + 4 * TILES)
            return (hs, hs[:, 0:SH].rearrange("p (m n) -> p m n", m=TILES),
                    hs[:, SH:SH + 2 * TILES].rearrange("p (m n) -> p m n", m=TILES),
                    hs[:, SH + 2 * TILES:].rearrange("p (m n) -> p m n", m=TILES))
        hs0, h, mv1, rr1 = h_parts("hs0")
        hs1 = h_parts("hs1")[0]
        hs2, h_m, mv_m, rr_m = h_parts("hs2")
        xT = sb("xT", PADT)
        nl = sb("nl", TILES, P)
        st1, vv1 = sb("st1", TILES, 6), sb("vv1", TILES, 2)
        hl = sb("hl", PADT + 1)
        d = sb("d", PADT)
        mixed = [sb("mixed0", PADT), sb("mixed1", PADT)]
        qk = [sb("qtok", TILES, P), sb("ktok", TILES, P)]
        rzx = sb("rzx", TILES, P)
        squared = [nl, rzx]
        ssq, nrm, rin = sb("ssq", 2, TILES), sb("nrm", 2, TILES), sb("rin", 2, TILES)
        v_f, gate_f = sb("v_f", TILES, P), sb("gate_f", PADT)
        q, k = sb("q", PADT), sb("k", PADT)
        zq = sb("zq", PADT)
        rz = sb("rz", TILES * HEADS)
        kc, kcT = sb("kc", NST * P), sb("kcT", NST, P)
        af = sb("af", HD * NST)

        v, gz = sb("v", TILES, P), sb("gz", PADT)
        ql = sb("ql", QCOLS - GRP)
        qx = sb("qx", 2, HEADS, QCOLS)
        ki, kh, ko, kw = (sb("ki", FOUR, 2 * GRP), sb("kh", 2 * GRP), sb("ko", NE - 1, 2 * GRP), sb("kw", NW - 1, 2 * GRP))
        qc = sb("qc", PADT)
        ab = sb("ab", NST, P)
        pd = [sb(f"pd{i}", HEADS * WIN) for i in range(2)]
        px = [sb(f"px{i}", HEADS, P) for i in range(2)]
        ga = sb("ga", PADT)

        x2, nl2, t_sum = sb("x2", TILES, P), sb("nl2", TILES, P), sb("t_sum", TILES, P)
        st2, mv2, vv2, rr2 = sb("st2", TILES, 6), sb("mv2", TILES, 2), sb("vv2", TILES), sb("rr2", TILES)
        st3, mv3, vv3, rr3 = sb("st3", TILES, 6), sb("mv3", TILES, 2), sb("vv3", TILES, 2), sb("rr3", TILES, 2)
        h1, n1, n2 = t_sum, nl2, x2
        c1, xa = sb("c1", PADT), sb("xa", PADT)
        hid = sb("hid", 4, PADT)

        bank = [ctx.enter_context(nc.psum_tensor(f"bank{i}", [P, 512], F32)) for i in range(8)]

        s_w = sem("s_w"); s_fc2 = sem("s_fc2"); s_zero = sem("s_zero"); s_init = sem("s_init"); s_clear = sem("s_clear")
        s_gp = sem("s_gp"); s_gc = sem("s_gc"); s_gd = sem("s_gd"); s_lam = sem("s_lam"); s_pw = sem("s_pw")
        s_tab = sem("s_tab")
        s_dec = sem("s_dec")
        x_in = sem("x_in")
        e_in = sem("e_in")
        qx_in = sem("qx_in")
        v_in = sem("v_in"); gz_in = sem("gz_in"); hs1_in = sem("hs1_in"); hs2_in = sem("hs2_in")
        o_out = sem("o_out")
        front = sem("front")
        rest = sem("rest")
        diag = sem("diag")
        off = sem("off")
        s_out = sem("s_out")
        h_cp = sem("h_cp"); hl_ok = sem("hl_ok")
        raw = sem("raw")
        v_ok = sem("v_ok"); th_ok = sem("th_ok"); eq = sem("eq"); ek = sem("ek"); kcT_ok = sem("kcT_ok")
        px_ok = sem("px_ok")
        n2T_ok = sem("n2T_ok"); n1T_ok = sem("n1T_ok"); nmT_ok = sem("nmT_ok"); fin_ok = sem("fin_ok")
        ge1 = sem("ge1"); ge2 = sem("ge2")
        bn1 = sem("bn1"); ag1 = sem("ag1"); var1 = sem("var1"); nl_ok = sem("nl_ok")
        nr_ok = sem("nr_ok"); ri_ok = sem("ri_ok"); tok = sem("tok")
        ql_ok = sem("ql_ok")
        kc_ok = sem("kc_ok"); z_ok = sem("z_ok"); qz_ok = sem("qz_ok"); rz_ok = sem("rz_ok")
        af_ok = sem("af_ok"); qc_ok = sem("qc_ok")
        gate_ok = sem("gate_ok"); ga_ok = sem("ga_ok")
        pd_ok = sem("pd_ok"); merged = sem("merged")
        aa_ok = sem("aa_ok")
        x2_ok = sem("x2_ok"); bn2 = sem("bn2"); ag2 = sem("ag2"); var2 = sem("var2"); nl2_ok = sem("nl2_ok")
        h1_ok = sem("h1_ok"); bn3 = sem("bn3"); ag3 = sem("ag3"); var3 = sem("var3"); n12_ok = sem("n12_ok")
        xa_ok = sem("xa_ok"); y_ok = sem("y_ok")
        r1_ok = sem("r1_ok"); rq_ok = sem("rq_ok"); r2_ok = sem("r2_ok"); r3_ok = sem("r3_ok"); t_ok = sem("t_ok")
        ab_ok = sem("ab_ok")
        d_ok = sem("d_ok"); mix = sem("mix")
        rzx_ok = sem("rzx_ok")
        kl_ok = sem("kl_ok")

        def nth(b, per, n):
            return b * per + n

        def first(b):
            return isinstance(b, int) and b == 0

        def before(eng, s, b, per, n):
            if not first(b):
                eng.wait_ge(s, (b - 1) * per + n)

        emptied = {"zt": (rz_ok, 1, 1), "u": (af_ok, 1, 1)}
        for g in (0, 1):
            for name, s in (("dct", h_cp), ("nT", hl_ok), ("v", v_ok), ("g", th_ok), ("qT", eq), ("kT", ek),
                            ("kc", kcT_ok), ("rT", gate_ok), ("wo", x2_ok), ("n2T", n2T_ok), ("w2_", h1_ok),
                            ("n1T", n1T_ok), ("nmT", nmT_ok), ("at", xa_ok), ("f2_", fin_ok), ("oT", y_ok)):
                emptied[f"{name}{g}"] = (s, 2, g + 1)
            emptied[f"q{g}"] = (raw, 4, g + 1)
            emptied[f"k{g}"] = (raw, 4, g + 3)
            for j in range(4):
                emptied[f"w1_{g}{j}"] = (ge1, 8, 4 * g + j + 1)
                emptied[f"f1_{g}{j}"] = (ge2, 8, 4 * g + j + 1)

        def free_bank(pe, b, order, banks, name):
            n = order.index(name)
            if n >= banks:
                s, per, i = emptied[order[n - banks]]
                pe.wait_ge(s, nth(b, per, i))
            else:
                last = max(j for j in range(len(order)) if j % banks == n)
                s, per, i = emptied[order[last]]
                before(pe, s, b, per, i)

        def bf(name):
            return bank[FRONT0 + FRONT.index(name) % 2]

        def bm(name):
            return bank[REST0 + REST.index(name) % 3]

        def front_bank(pe, b, name):
            free_bank(pe, b, FRONT, 2, name)
            return bf(name)

        def rest_bank(pe, b, name):
            free_bank(pe, b, REST, 3, name)
            return bm(name)

        def used(b, name):
            return nth(b, len(FRONT), FRONT.index(name) + 1)

        def used_m(b, name):
            return nth(b, len(REST), REST.index(name) + 1)

        def last_use(eng, b, g):
            if g >= 2:
                eng.wait_ge(off, nth(b, TILES, 2 * g - 2))
            else:
                before(eng, off, b, TILES, 2 * g + 6)

        def rounds(eng, body):
            def at(n):
                return [n - d if 0 <= n - d < B else None for d in range(4)]
            for n in range(3):
                body(*at(n))
            with eng.Fori(3, B) as i:
                body(i, i - 1, i - 2, i - 3)
            for n in range(B, B + 3):
                body(*at(n))

        def cols(g):
            return slice(HALF * g, HALF * g + width[g])

        def tiles(g):
            return range(4 * g, 4 * g + 4)

        def over(ap, n, m):
            return ap.rearrange("p (o m) -> p o m", o=1).to_broadcast([P, n, m])

        block = ctx.enter_context(nc.Block())

        @block.sync
        def _(sp):
            G = qx[:, :, :, :].rearrange("p g h n -> p (g h n)")[:, 0:E * (4 * P + 1)].rearrange("p (e n) -> p e n", e=E)
            loads = [(dct, A["dct"]), (ident, A["ident"]), (heads1, A["heads1"]), (mask, A["mask"]),
                     (wq, A["wqT"]), (wk, A["wkT"]), (wv, A["wvT"]), (wg, A["wgT"]), (wo, A["woT"]),
                     (wat, A["watT"]), (w1, A["w1T"])]
            sp.dma_start(hid[:, :, :].rearrange("p j (a n) -> p (j a) n", a=2), A["fc2"].rearrange("e d n -> d e n")).then_inc(s_fc2, 16)
            for dst, src in ((wnext, A["wnextT"]), (fc2b, A["fc2bT"]), (vec, A["vec"])):
                sp.dma_start(dst[:, :], src).then_inc(s_fc2, 16)

            def samples(b, at):
                if not first(b):
                    sp.wait_ge(front, used(b - 1, "dct1"))
                sp.dma_start(xT[:, 0:full], A["xT"][at, :, :]).then_inc(x_in, 16)
                sp.dma_start(xT[0:TAIL, full:T], A["xtail"][at, :].rearrange("(p o) -> p o", o=1)).then_inc(x_in, 16)

            sp.wait_ge(s_zero, 1)
            samples(0, 0)
            for dst, src in loads:
                sp.dma_start(dst[:, :], src).then_inc(s_w, 16)
            sp.dma_start(w2[:, :, :], A["w2T"].rearrange("(j p) n -> p j n", p=P)).then_inc(s_w, 16)
            sp.wait_ge(s_gc, E + 1)
            sp.dma_start(g_dram.rearrange("e p n -> p e n"), G).then_inc(s_gd, 16)
            sp.wait_ge(s_gd, 16)

            def expert(m):
                e = m % E
                before(sp, fin_ok, m, 2, 2)
                sp.dma_start(f1w[:, :], A["fc1T"][e, :, :]).then_inc(e_in, 16)
                sp.dma_start(f1b[:, :], A["fc1b"][e, :, :]).then_inc(e_in, 16)
                sp.dma_start(f2w[:, :], g_dram[e, :, :]).then_inc(e_in, 16)

            def spread(b, g):
                if first(b) and g == 0:
                    sp.wait_ge(s_clear, 1)
                sp.wait_ge(ql_ok, nth(b, GROUPS, g + 1))
                for hd in range(HEADS):
                    rows = slice(HD * hd, HD * hd + HD)
                    sp.dma_start(qx[rows, g % 2, hd, 0:scan_w[g]], q[rows, GRP * g:GRP * g + scan_w[g]]).then_inc(qx_in, 16)
                    sp.dma_start(qx[rows, g % 2, hd, GRP:QCOLS], ql[rows, :]).then_inc(qx_in, 16)

            def hand_v(s):
                before(sp, s_out, s, TILES, TILES)
                sp.dma_start(v[:, :, :], v_f[:, :, :]).then_inc(v_in, 16)

            def hand_gate(s):
                sp.wait_ge(gate_ok, nth(s, 2, 2))
                sp.dma_start(gz[:, :], gate_f[:, :]).then_inc(gz_in, 16)

            def hand_h(f, s, m):
                if s is not None:
                    if m is not None:
                        sp.wait_ge(t_ok, nth(m, 2, 2))
                    sp.dma_start(hs2[:, :], hs1[:, :]).then_inc(hs2_in, 16)
                if f is not None:
                    if s is not None:
                        handed, there = nth(s, 16, 16), nth(f, 2, 2)
                        sp.wait_ge(hs2_in, handed)
                        sp.wait_ge(nl_ok, there)
                    else:
                        sp.wait_ge(nl_ok, nth(f, 2, 2))
                    sp.dma_start(hs1[:, :], hs0[:, :]).then_inc(hs1_in, 16)

            def store(p, g):
                sp.wait_ge(y_ok, nth(p, 2, g + 1))
                r0 = HALF * g
                whole = 4 - g
                sp.dma_start(out[p, r0:r0 + whole * P, :].rearrange("(m p) n -> p m n", p=P),
                             h1[:, 4 * g:4 * g + whole, :]).then_inc(o_out, 16)
                if g:
                    sp.dma_start(out[p, (TILES - 1) * P:T, :], h1[0:last_rows, TILES - 1, :]).then_inc(o_out, 16)

            def body(f, s, m, t):
                if s is not None:
                    hand_v(s); spread(s, 1); hand_gate(s)
                if f is not None:
                    samples(f + 1, (f + 1) % B)
                if t is not None:
                    store(t, 0); store(t, 1)
                if m is not None:
                    expert(m)
                if s is not None:
                    spread(s, 2); spread(s, 3)
                if f is not None or s is not None:
                    hand_h(f, s, m)
                if f is not None:
                    spread(f, 0)
            rounds(sp, body)
            sp.wait_ge(o_out, 48 * B)

        @block.gpsimd
        def _(gp):
            gp.memset(xT[:, :], 0.0).then_inc(s_zero, 1)
            for tile in (nhalf, phalf):
                gp.memset(tile[:, :], -0.5 if tile is nhalf else 0.5)
            gp.memset(zq[:, :], 1.0)
            for tile in (hl, mixed[0], mixed[1]):
                gp.memset(tile[:, :], 0.0)
            gp.memset(px[0][:, :, :], 0.0)
            gp.memset(px[1][:, :, :], 0.0).then_inc(s_init, 1)
            gp.wait_ge(s_tab, 1)
            gp.wait_ge(s_init, 2)

            def clear():
                gp.wait_ge(s_gc, E)
                gp.memset(hid[:, :, :], 0.0)
                gp.wait_ge(s_gd, 16)
                gp.memset(qx[:, :, :, :], 0.0).then_inc(s_clear, 1)

            def pow1(a, g):
                gp.wait_ge(var1, nth(a, 2, g + 1))
                gp.tensor_tensor(rr1[:, 4 * g:4 * g + 4, :], vv1[:, 4 * g:4 * g + 4, :],
                                 nhalf[:, 0:8].rearrange("p (m o) -> p m o", o=2), ALU.pow).then_inc(r1_ok, 1)

            def powq(a, i):
                gp.wait_ge(raw, nth(a, 4, 2 * i + 2))
                gp.tensor_tensor(nrm[:, i, :], ssq[:, i, :], phalf[:, 0:TILES], ALU.pow).then_inc(rq_ok, 1)

            def klev(b, g):
                gp.wait_ge(ek, nth(b, 2, g // 2 + 1))
                last_use(gp, b, g)
                parts = [(ki[:, 0, :], FOUR, 1, 0)]
                parts += [(ki[:, j, :], FOUR, j + 1, j) for j in range(1, FOUR)]
                parts += [(kh[:, :], EIGHT, FOUR, FOUR)]
                parts += [(ko[:, j - 1, :], WIN, EIGHT * j, EIGHT * j) for j in range(1, NE)]
                parts += [(kw[:, w - 1, :], P, WIN * w, WIN * w) for w in range(1, NW)]
                for dst, m, n, ref in parts:
                    w = GRP if m == P else scan_w[g]
                    view = lambda ap: ap.rearrange("p (x m) -> p x m", m=m)[:, :, 0:n]
                    last = gp.tensor_tensor(view(dst[:, GRP * (g % 2):GRP * (g % 2) + w]), view(k[:, GRP * g:GRP * g + w]),
                                            over(rp[:, P - ref:P - ref + n], w // m, n), ALU.mult)
                last.then_inc(kl_ok, 1)

            def states(b):
                gp.wait_ge(af_ok, nth(b, 1, 1))
                before(gp, s_out, b, TILES, TILES)
                wide = [P, NST, HEADS, HD]
                gp.tensor_tensor(ab[:, :, :].rearrange("p c (h e) -> p c h e", h=HEADS),
                                 af[:, :].rearrange("p (o e c) -> p c o e", o=1, e=HD).to_broadcast(wide),
                                 heads1[:, :].rearrange("p (o h e) -> p o h e", o=1, h=HEADS).to_broadcast(wide), ALU.mult).then_inc(ab_ok, 1)

            def pow2(p, g):
                gp.wait_ge(var2, nth(p, 2, g + 1))
                gp.tensor_tensor(rr2[:, 4 * g:4 * g + 4], vv2[:, 4 * g:4 * g + 4], nhalf[:, 0:4], ALU.pow).then_inc(r2_ok, 1)

            def resid(p, g):
                before(gp, o_out, p, 48, 48)
                gp.wait_ge(x2_ok, nth(p, 2, g + 1))
                gp.tensor_tensor(t_sum[:, 4 * g:4 * g + 4, :], x2[:, 4 * g:4 * g + 4, :], h_m[:, 4 * g:4 * g + 4, :],
                                 ALU.add).then_inc(t_ok, 1)

            def pow3(p, g):
                gp.wait_ge(var3, nth(p, 2, g + 1))
                gp.tensor_tensor(rr3[:, 4 * g:4 * g + 4, :], vv3[:, 4 * g:4 * g + 4, :],
                                 nhalf[:, 0:8].rearrange("p (m o) -> p m o", o=2), ALU.pow).then_inc(r3_ok, 1)

            def body(f, s, m, t):
                if s is not None:
                    klev(s, 1)
                if f is not None:
                    pow1(f, 0); pow1(f, 1)
                if s is not None:
                    states(s)
                if m is not None:
                    pow2(m, 0); pow2(m, 1)
                if s is not None:
                    klev(s, 2)
                if m is not None:
                    resid(m, 0); resid(m, 1)
                if f is not None:
                    powq(f, 0); powq(f, 1)
                    if first(f):
                        clear()
                if s is not None:
                    klev(s, 3)
                if m is not None:
                    pow3(m, 0); pow3(m, 1)
                if f is not None:
                    klev(f, 0)
            rounds(gp, body)

        @block.scalar
        def _(act):
            G = qx[:, :, :, :].rearrange("p g h n -> p (g h n)")[:, 0:E * (4 * P + 1)].rearrange("p (e n) -> p e n", e=E)
            for e in range(E):
                act.wait_ge(s_gp, e + 1)
                nc.scalar.activation(G[:, e, 0:4 * P], bank[e][:, :], ACT.Copy).then_inc(s_gc, 1)
            act.wait_ge(s_fc2, 4 * 16)
            act.wait_ge(s_gp, E + 1)
            nc.scalar.activation(G[:, :, 4 * P], bank[0][:, 0:E], ACT.Identity, bias=col("nx_b")).then_inc(s_gc, 1)
            act.wait_ge(s_init, 2)
            nc.scalar.activation(lam[:, 0:1], col("td"), ACT.Exp).then_inc(s_lam, 1)
            act.wait_ge(s_lam, 1)
            nc.scalar.activation(lam[:, 1:2], lam[:, 0:1], ACT.Exp, scale=-1.0).then_inc(s_lam, 1)

            def hcopy(a, g):
                act.wait_ge(front, used(a, f"dct{g}"))
                before(act, hs1_in, a, 16, 16)
                nc.scalar.activation(h[:, 4 * g:4 * g + 4, :], bf(f"dct{g}")[:, :].rearrange("p (m n) -> p m n", m=4), ACT.Copy).then_inc(h_cp, 1)

            def spread_rz(s):
                act.wait_ge(rz_ok, nth(s, 1, 1))
                nc.scalar.activation(rzx[:, :, :].rearrange("p m (h n) -> p (m h) n", h=HEADS),
                                     rz[:, :].rearrange("p (m o) -> p m o", o=1).to_broadcast([P, TILES * HEADS, HD]),
                                     ACT.Copy).then_inc(rzx_ok, 1)

            def hlT(a, g):
                act.wait_ge(front, used(a, f"nT{g}"))
                nc.scalar.activation(hl[:, 1 + HALF * g:1 + HALF * g + width[g]], bf(f"nT{g}")[:, 0:width[g]], ACT.Identity,
                                     scale=col("ln1_g"), bias=col("ln1_b")).then_inc(hl_ok, 1)

            def squares(a, i, g):
                name = f"{'qk'[i]}{g}"
                act.wait_ge(front, used(a, name))
                nc.scalar.activation(qk[i][:, 4 * g:4 * g + 4, :], bf(name)[:, :].rearrange("p (m n) -> p m n", m=4), ACT.Copy)
                for m in range(4):
                    last = nc.scalar.activation(squared[i][:, 4 * g + m, :], bf(name)[:, P * m:P * m + P], ACT.Square,
                                                accum_out=ssq[:, i, 4 * g + m:4 * g + m + 1])
                last.then_inc(raw, 1)

            def vcopy(a, g):
                act.wait_ge(front, used(a, f"v{g}"))
                before(act, v_in, a, 16, 16)
                nc.scalar.activation(v_f[:, 4 * g:4 * g + 4, :], bf(f"v{g}")[:, :].rearrange("p (m n) -> p m n", m=4), ACT.Copy).then_inc(v_ok, 1)

            def gate(a, g):
                act.wait_ge(front, used(a, f"g{g}"))
                before(act, gz_in, a, 16, 16)
                nc.scalar.activation(gate_f[:, cols(g)], bf(f"g{g}")[:, 0:width[g]], ACT.Tanh, scale=0.5).then_inc(th_ok, 1)

            def exps(a, i, g):
                name = f"{'qk'[i]}T{g}"
                act.wait_ge(front, used(a, name))
                if i == 0:
                    before(act, qx_in, a, 512, 512)
                    before(act, qc_ok, a, 1, 1)
                else:
                    before(act, kl_ok, a, GROUPS, GROUPS)
                nc.scalar.activation((q, k)[i][:, cols(g)], bf(name)[:, 0:width[g]], ACT.Exp,
                                     scale=col("rms")).then_inc((eq, ek)[i], 1)

            def kcopy(a, g):
                n = (4, NST - 4)[g]
                act.wait_ge(front, used(a, f"kc{g}"))
                nc.scalar.activation(kcT[:, 4 * g:4 * g + n, :], bf(f"kc{g}")[:, 0:P * n].rearrange("p (m n) -> p m n", m=n), ACT.Copy).then_inc(kcT_ok, 1)

            def pxs(a, c):
                X, O, n = px[c % 2], bank[BETWEEN], windows[c]
                if c >= 2:
                    act.wait_ge(s_out, nth(a, TILES, c - 1))
                else:
                    before(act, s_out, a, TILES, TILES - 1 + c)
                act.wait_ge(off, nth(a, TILES, c + 1))
                for w in range(1, n):
                    nc.scalar.activation(X[0:WIN * w, :, WIN * w:WIN * w + WIN],
                                         O[0:WIN * w, SW * (w - 1):SW * w].rearrange("p (h n) -> p h n", h=HEADS), ACT.Copy)
                act.wait_ge(pd_ok, nth(a, TILES, c + 1))
                for w in range(n):
                    r = slice(WIN * w, WIN * w + WIN)
                    last = nc.scalar.activation(X[r, :, r], pd[c % 2][r, :].rearrange("p (h n) -> p h n", h=HEADS), ACT.Copy)
                last.then_inc(px_ok, 1)

            def n2T(p, g):
                act.wait_ge(rest, used_m(p, f"n2T{g}"))
                nc.scalar.activation(c1[:, cols(g)], bm(f"n2T{g}")[:, 0:width[g]], ACT.Identity,
                                     scale=col("ln2_g"), bias=col("ln2_b")).then_inc(n2T_ok, 1)

            def gelu1(p, g):
                for j in range(4):
                    act.wait_ge(rest, used_m(p, f"w1_{g}{j}"))
                    nc.scalar.activation(hid[:, j, cols(g)], bm(f"w1_{g}{j}")[:, 0:width[g]], ACT.Gelu).then_inc(ge1, 1)

            def nT(p, g):
                act.wait_ge(rest, used_m(p, f"n1T{g}"))
                nc.scalar.activation(xa[:, cols(g)], bm(f"n1T{g}")[:, 0:width[g]], ACT.Copy).then_inc(n1T_ok, 1)
                act.wait_ge(rest, used_m(p, f"nmT{g}"))
                nc.scalar.activation(c1[:, cols(g)], bm(f"nmT{g}")[:, 0:width[g]], ACT.Identity,
                                     scale=col("f_g"), bias=col("f_b")).then_inc(nmT_ok, 1)

            def gelu2(p, g):
                act.wait_ge(e_in, nth(p, 48, 48))
                for j in range(4):
                    act.wait_ge(rest, used_m(p, f"f1_{g}{j}"))
                    nc.scalar.activation(hid[:, j, cols(g)], bm(f"f1_{g}{j}")[:, 0:width[g]], ACT.Gelu,
                                         bias=f1b[:, j:j + 1]).then_inc(ge2, 1)

            def fin(p, g):
                act.wait_ge(rest, used_m(p, f"f2_{g}"))
                nc.scalar.activation(c1[:, cols(g)], bm(f"f2_{g}")[:, 0:width[g]], ACT.Gelu,
                                     bias=f2w[:, 4 * P:4 * P + 1]).then_inc(fin_ok, 1)

            def body(f, s, m, t):
                if s is not None:
                    spread_rz(s); pxs(s, 0)
                if f is not None:
                    hcopy(f, 0); hcopy(f, 1)
                if t is not None:
                    gelu2(t, 1); fin(t, 1)
                if s is not None:
                    pxs(s, 1)
                if f is not None:
                    hlT(f, 0); hlT(f, 1)
                if s is not None:
                    pxs(s, 2)
                if f is not None:
                    squares(f, 0, 0); squares(f, 0, 1)
                if m is not None:
                    n2T(m, 0)
                if f is not None:
                    squares(f, 1, 0); squares(f, 1, 1)
                if m is not None:
                    n2T(m, 1); gelu1(m, 0)
                if s is not None:
                    pxs(s, 3)
                if m is not None:
                    gelu1(m, 1)
                if f is not None:
                    vcopy(f, 0); vcopy(f, 1)
                if s is not None:
                    pxs(s, 4)
                if f is not None:
                    exps(f, 0, 0); exps(f, 0, 1)
                if s is not None:
                    pxs(s, 5)
                if f is not None:
                    exps(f, 1, 0); exps(f, 1, 1); gate(f, 0); gate(f, 1)
                    kcopy(f, 0); kcopy(f, 1)
                if m is not None:
                    nT(m, 0)
                if s is not None:
                    pxs(s, 6)
                if m is not None:
                    nT(m, 1); gelu2(m, 0)
                if s is not None:
                    pxs(s, 7)
                if m is not None:
                    fin(m, 0)
            rounds(act, body)

        @block.vector
        def _(dve):
            V = nc.vector
            V.memset(zeros[:, :], 0.0)
            V.memset(pw[:, 0:1], 1.0)
            V.memset(dec[:, :, :], 0.0).then_inc(s_pw, 1)
            for tile in (q, k, qc, ga, kh, ql, gate_f, pd[0], pd[1], c1, xa):
                V.memset(tile[:, :], 0.0)
            for tile in (ki, ko, kw):
                last = V.memset(tile[:, :, :], 0.0)
            last.then_inc(s_init, 1)
            dve.wait_ge(s_pw, 1)
            dve.wait_ge(s_lam, 2)
            V.tensor_tensor_scan(pw[:, 1:P + 1], lam[:, 1:2].to_broadcast([P, P]), zeros[:, :], 1.0, ALU.mult, ALU.add).then_inc(s_pw, 1)
            dve.wait_ge(s_pw, 2)
            V.tensor_copy(dec[:, :, 1:NST], over(pw[:, P:P + 1], HD, 1).to_broadcast([P, HD, NST - 1])).then_inc(s_dec, 1)
            V.tensor_copy(rp[:, :], pw[:, P::-1]).then_inc(s_tab, 1)
            dve.wait_ge(s_tab, 1)
            dve.wait_ge(s_dec, 1)
            dve.wait_ge(s_init, 2)

            def stats(src, st, mv, bn, ag, b, g):
                for m in tiles(g):
                    last = V.bn_stats(st[:, m, :], src[:, m, :])
                last.then_inc(bn, 1)
                dve.wait_ge(bn, nth(b, 2, g + 1))
                V.memset(tick[:, :], 0.0)
                for m in tiles(g):
                    last = V.bn_aggr(mv[:, m, :], st[:, m, :])
                last.then_inc(ag, 1)
                dve.wait_ge(ag, nth(b, 2, g + 1))

            def twice_normed(vv, mv, g):
                s = slice(4 * g, 4 * g + 4)
                V.tensor_scalar(vv[:, s, 0], mv[:, s, 1], EPS, None, ALU.add)
                return V.tensor_scalar(vv[:, s, 1], mv[:, s, 1], 1.0 + EPS, EPS * EPS, ALU.mult, ALU.add)

            def ln1(a, g):
                dve.wait_ge(h_cp, nth(a, 2, g + 1))
                stats(h, st1, mv1, bn1, ag1, a, g)
                twice_normed(vv1, mv1, g).then_inc(var1, 1)

            def normed(a, g):
                dve.wait_ge(r1_ok, nth(a, 2, g + 1))
                for m in tiles(g):
                    last = V.tensor_scalar(nl[:, m, :], h[:, m, :], mv1[:, m, 0:1], rr1[:, m, 1:2], ALU.subtract, ALU.mult)
                last.then_inc(nl_ok, 1)

            def mixes(f, i):
                if i == 0:
                    dve.wait_ge(hl_ok, nth(f, 2, 2))
                    V.tensor_tensor(d[:, 0:T], hl[:, 1:T + 1], hl[:, 0:T], ALU.subtract).then_inc(d_ok, 1)
                    dve.wait_ge(d_ok, nth(f, 1, 1))
                if i >= 2:
                    dve.wait_ge(front, used(f, ("q1", "k1")[i - 2]))
                V.scalar_tensor_tensor(mixed[i % 2][:, 0:T], d[:, 0:T], col(("tm_q", "tm_k", "tm_v", "tm_g")[i]), hl[:, 0:T],
                                       ALU.mult, ALU.add).then_inc(mix, 1)

            def tokens(a, i):
                dve.wait_ge(rq_ok, nth(a, 2, i + 1))
                V.tensor_scalar(nrm[:, i, :], nrm[:, i, :], P ** -0.5, 1e-8, ALU.mult, ALU.add).then_inc(nr_ok, 1)
                dve.wait_ge(nr_ok, nth(a, 2, i + 1))
                V.reciprocal(rin[:, i, :], nrm[:, i, :]).then_inc(ri_ok, 1)
                dve.wait_ge(ri_ok, nth(a, 2, i + 1))
                for m in range(TILES):
                    last = V.tensor_scalar(qk[i][:, m, :], qk[i][:, m, :], rin[:, i, m:m + 1], None, ALU.mult)
                last.then_inc(tok, 1)

            def qlev(b, g):
                dve.wait_ge(eq, nth(b, 2, g // 2 + 1))
                last_use(dve, b, g)
                if g:
                    dve.wait_ge(qx_in, nth(b, 512, 128 * g))
                else:
                    before(dve, qx_in, b, 512, 512)
                src, w = q[:, GRP * g:GRP * g + scan_w[g]], scan_w[g]
                for at, m, n in ((Q8, EIGHT, 0), (Q32, WIN, 0), (Q4, EIGHT, FOUR)):
                    view = lambda ap, m: ap.rearrange("p (x m) -> p x m", m=m)
                    dst = ql[:, at - GRP:at - GRP + w * (m - n) // m]
                    last = V.tensor_tensor(view(dst, m - n), view(src, m)[:, :, n:m], over(pw[:, 0:m - n], w // m, m - n), ALU.mult)
                last.then_inc(ql_ok, 1)

            def inter(f):
                dve.wait_ge(ek, nth(f, 2, 2))
                V.tensor_tensor(kc[:, :].rearrange("p (n m) -> p n m", n=NST),
                                k[:, 0:NST * P].rearrange("p (n m) -> p n m", n=NST), over(rp[:, 1:P + 1], NST, P), ALU.mult).then_inc(kc_ok, 1)
                V.tensor_tensor_scan(zq[:, 0:T], lam[:, 1:2].to_broadcast([P, T]), k[:, 0:T], 0.0, ALU.mult, ALU.add).then_inc(z_ok, 1)
                dve.wait_ge(z_ok, nth(f, 1, 1))
                V.tensor_tensor(zq[:, 0:T], q[:, 0:T], zq[:, 0:T], ALU.mult).then_inc(qz_ok, 1)

            def from_start(s):
                before(dve, s_out, s, TILES, TILES)
                V.tensor_tensor(qc[:, :].rearrange("p (n m) -> p n m", n=TILES),
                                q[:, :].rearrange("p (n m) -> p n m", n=TILES), over(pw[:, 1:P + 1], TILES, P), ALU.mult).then_inc(qc_ok, 1)

            def denominators(f):
                dve.wait_ge(front, used(f, "zt"))
                V.reciprocal(rz[:, :], bf("zt")[:, 0:TILES * HEADS]).then_inc(rz_ok, 1)

            def gates(s, g):
                dve.wait_ge(front, used(s, f"rT{g}"))
                V.scalar_tensor_tensor(gate_f[:, cols(g)], gate_f[:, cols(g)], 1.0, bf(f"rT{g}")[:, 0:width[g]], ALU.add, ALU.mult).then_inc(gate_ok, 1)

            def chain(f):
                dve.wait_ge(front, used(f, "u"))
                before(dve, ab_ok, f, 1, 1)
                V.tensor_tensor_scan(af[:, :], dec[:, :, :].rearrange("p e c -> p (e c)"), bf("u")[:, 0:HD * NST],
                                     0.0, ALU.mult, ALU.add).then_inc(af_ok, 1)

            def merge(a, c):
                D, rows = bank[DIAG], WIN * windows[c]
                dve.wait_ge(diag, nth(a, TILES, c + 1))
                if c >= 2:
                    dve.wait_ge(px_ok, nth(a, TILES, c - 1))
                else:
                    before(dve, px_ok, a, TILES, TILES - 1 + c)
                n = 2 * TILES
                heads = lambda ap, m: ap.rearrange("p (h m) -> p h m", h=HEADS)
                pdc = pd[c % 2][0:rows, :]
                V.tensor_copy(heads(pdc, WIN)[:, :, EIGHT:WIN], heads(D[0:rows, SW:2 * SW], WIN)[:, :, EIGHT:WIN]).then_inc(merged, 1)
                dve.wait_ge(merged, nth(a, n, 2 * c + 1))
                V.memset(tick[:, :], 0.0)
                V.copy_predicated(pdc, mask[0:rows, 0:SW], D[0:rows, 0:SW]).then_inc(merged, 1)
                dve.wait_ge(merged, nth(a, n, 2 * c + 2))
                V.memset(tick[:, :], 0.0)
                V.copy_predicated(pdc.rearrange("p (x m) -> p x m", m=EIGHT)[:, :, FOUR:EIGHT],
                                  mask[0:rows, SW:SW + SW // 2].rearrange("p (x m) -> p x m", m=FOUR),
                                  D[0:rows, 2 * SW:2 * SW + SW // 2].rearrange("p (x m) -> p x m", m=FOUR)).then_inc(pd_ok, 1)

            def gated(a, g):
                dve.wait_ge(s_out, nth(a, TILES, 4 * g + 4))
                dve.wait_ge(gz_in, nth(a, 16, 16))
                before(dve, rest, a, len(REST), REST.index(f"wo{g}") + 1)
                V.scalar_tensor_tensor(ga[:, cols(g)], bank[SOUT][:, 0:width[g]], 0.5, gz[:, cols(g)], ALU.mult, ALU.mult).then_inc(ga_ok, 1)

            def attn_in(m):
                dve.wait_ge(hs2_in, nth(m, 16, 16))
                for i in range(TILES):
                    last = V.tensor_scalar(x2[:, i, :], h_m[:, i, :], mv_m[:, i, 0:1], rr_m[:, i, 0:1], ALU.subtract, ALU.mult)
                last.then_inc(aa_ok, 1)

            def attended(p, g):
                dve.wait_ge(rest, used_m(p, f"wo{g}"))
                dve.wait_ge(aa_ok, nth(p, 1, 1))
                s = slice(4 * g, 4 * g + 4)
                V.tensor_tensor(x2[:, s, :], bm(f"wo{g}")[:, :].rearrange("p (m n) -> p m n", m=4), x2[:, s, :], ALU.add).then_inc(x2_ok, 1)
                dve.wait_ge(x2_ok, nth(p, 2, g + 1))
                stats(x2, st2, mv2, bn2, ag2, p, g)
                V.tensor_scalar(vv2[:, s], mv2[:, s, 1], EPS, None, ALU.add).then_inc(var2, 1)

            def normed2(p, g):
                dve.wait_ge(r2_ok, nth(p, 2, g + 1))
                for m in tiles(g):
                    last = V.tensor_scalar(nl2[:, m, :], x2[:, m, :], mv2[:, m, 0:1], rr2[:, m:m + 1], ALU.subtract, ALU.mult)
                last.then_inc(nl2_ok, 1)

            def hidden(p, g):
                dve.wait_ge(rest, used_m(p, f"w2_{g}"))
                dve.wait_ge(t_ok, nth(p, 2, g + 1))
                s = slice(4 * g, 4 * g + 4)
                V.tensor_tensor(h1[:, s, :], bm(f"w2_{g}")[:, :].rearrange("p (m n) -> p m n", m=4), t_sum[:, s, :], ALU.add).then_inc(h1_ok, 1)
                dve.wait_ge(h1_ok, nth(p, 2, g + 1))
                stats(h1, st3, mv3, bn3, ag3, p, g)
                twice_normed(vv3, mv3, g).then_inc(var3, 1)

            def normed3(p, g):
                dve.wait_ge(r3_ok, nth(p, 2, g + 1))
                dve.wait_ge(rest, used_m(p, f"n2T{g}"))
                for m in tiles(g):
                    V.tensor_scalar(n1[:, m, :], h1[:, m, :], mv3[:, m, 0:1], rr3[:, m, 0:1], ALU.subtract, ALU.mult)
                    last = V.tensor_scalar(n2[:, m, :], h1[:, m, :], mv3[:, m, 0:1], rr3[:, m, 1:2], ALU.subtract, ALU.mult)
                last.then_inc(n12_ok, 1)

            def x_attn(p, g):
                dve.wait_ge(rest, used_m(p, f"at{g}"))
                dve.wait_ge(n1T_ok, nth(p, 2, g + 1))
                V.scalar_tensor_tensor(xa[:, cols(g)], bm(f"at{g}")[:, 0:width[g]], col("at_b"), xa[:, cols(g)], ALU.add, ALU.add).then_inc(xa_ok, 1)

            def result(p, g):
                dve.wait_ge(rest, used_m(p, f"oT{g}"))
                s = slice(4 * g, 4 * g + 4)
                V.tensor_tensor(h1[:, s, :], bm(f"oT{g}")[:, :].rearrange("p (m n) -> p m n", m=4), h1[:, s, :], ALU.add).then_inc(y_ok, 1)

            def body(f, s, m, t):
                if s is not None:
                    merge(s, 0); qlev(s, 1); gates(s, 0); gates(s, 1)
                if t is not None:
                    result(t, 0)
                if f is not None:
                    ln1(f, 0); ln1(f, 1)
                if s is not None:
                    from_start(s)
                if f is not None:
                    normed(f, 0); normed(f, 1)
                if s is not None:
                    merge(s, 1)
                if m is not None:
                    attn_in(m)
                if t is not None:
                    result(t, 1)
                if m is not None:
                    attended(m, 0)
                if f is not None:
                    mixes(f, 0); mixes(f, 1)
                if m is not None:
                    attended(m, 1)
                if s is not None:
                    merge(s, 2)
                if m is not None:
                    normed2(m, 0); normed2(m, 1)
                if s is not None:
                    qlev(s, 2); merge(s, 3)
                if f is not None:
                    mixes(f, 2); tokens(f, 0); mixes(f, 3); tokens(f, 1)
                if s is not None:
                    qlev(s, 3); merge(s, 4); gated(s, 0); merge(s, 5)
                if m is not None:
                    hidden(m, 0)
                if f is not None:
                    inter(f)
                if m is not None:
                    hidden(m, 1); normed3(m, 0)
                if s is not None:
                    merge(s, 6)
                if m is not None:
                    normed3(m, 1); x_attn(m, 0)
                if f is not None:
                    qlev(f, 0)
                if m is not None:
                    x_attn(m, 1)
                if s is not None:
                    merge(s, 7)
                if f is not None:
                    chain(f); denominators(f)
                if s is not None:
                    gated(s, 1)
            rounds(dve, body)

        @block.tensor
        def _(pe):
            mm = nc.tensor.matmul
            pe.wait_ge(s_fc2, 4 * 16)
            fc2 = hid[:, :, :].rearrange("p j (a n) -> p (j a) n", a=2)
            for e in range(E):
                for j in range(4):
                    last = mm(bank[e][:, P * j:P * j + P], fc2[:, e, P * j:P * j + P], wnext[:, :], start=True, stop=True)
                last.then_inc(s_gp, 1)
            pe.wait_ge(s_gc, 1)
            mm(bank[0][:, 0:E], wnext[:, :], fc2b[:, :], start=True, stop=True).then_inc(s_gp, 1)
            pe.wait_ge(s_gc, E + 1)
            pe.wait_ge(s_w, 12 * 16)
            pe.wait_ge(s_init, 2)

            def product(bk, src, w, g):
                for i, m in enumerate(tiles(g)):
                    last = mm(bk[:, P * i:P * i + P], src[:, P * m:P * m + P], w[:, :], start=True, stop=True)
                return last

            def transposed(bk, src, ms):
                for i, m in enumerate(ms):
                    last = nc.tensor.transpose(bk[:, P * i:P * i + P], src(m), ident[:, :])
                return last

            def dcts(a, g):
                bk = front_bank(pe, a, f"dct{g}")
                pe.wait_ge(x_in, nth(a, 32, 32))
                product(bk, xT, dct, g).then_inc(front, 1)

            def nTs(a, g):
                bk = front_bank(pe, a, f"nT{g}")
                pe.wait_ge(nl_ok, nth(a, 2, g + 1))
                transposed(bk, lambda m: nl[:, m, :], tiles(g)).then_inc(front, 1)

            def qkv(a, name, g):
                i = "qkv".index(name)
                bk = front_bank(pe, a, f"{name}{g}")
                pe.wait_ge(mix, nth(a, 4, i + 1))
                product(bk, mixed[i % 2], (wq, wk, wv)[i], g).then_inc(front, 1)

            def gates(a, g):
                bk = front_bank(pe, a, f"g{g}")
                pe.wait_ge(mix, nth(a, 4, 4))
                mm(bk[:, 0:width[g]], wg[:, :], mixed[1][:, cols(g)], start=True, stop=True).then_inc(front, 1)

            def qkTs(a, i, g):
                bk = front_bank(pe, a, f"{'qk'[i]}T{g}")
                pe.wait_ge(tok, nth(a, 2, i + 1))
                transposed(bk, lambda m: qk[i][:, m, :], tiles(g)).then_inc(front, 1)

            def kcs(a, g):
                bk = front_bank(pe, a, f"kc{g}")
                pe.wait_ge(kc_ok, nth(a, 1, 1))
                transposed(bk, lambda m: kc[:, P * m:P * m + P], range(4 * g, min(4 * g + 4, NST))).then_inc(front, 1)

            def zts(a):
                bk = front_bank(pe, a, "zt")
                pe.wait_ge(qz_ok, nth(a, 1, 1))
                for m in range(TILES):
                    last = mm(bk[:, HEADS * m:HEADS * m + HEADS], zq[:, P * m:P * m + P], heads1[:, 0:P:HD], start=True, stop=True)
                last.then_inc(front, 1)

            def rTs(a, g):
                bk = front_bank(pe, a, f"rT{g}")
                pe.wait_ge(rzx_ok, nth(a, 1, 1))
                transposed(bk, lambda m: rzx[:, m, :], tiles(g)).then_inc(front, 1)

            def us(f):
                bk = front_bank(pe, f, "u")
                pe.wait_ge(kcT_ok, nth(f, 2, 2))
                pe.wait_ge(v_ok, nth(f, 2, 2))
                for c in range(NST):
                    for hd in range(HEADS):
                        r = slice(HD * hd, HD * hd + HD)
                        last = mm(bk[r, c:HD * NST:NST], kcT[:, c, r], v_f[:, c, r], start=True, stop=True)
                last.then_inc(front, 1)

            def pairs(b, c):
                g, n, x = c // 2, windows[c], qx[:, c // 2 % 2, :, :]
                D, O = bank[DIAG], bank[BETWEEN]
                if c:
                    pe.wait_ge(pd_ok, nth(b, TILES, c))
                else:
                    before(pe, pd_ok, b, TILES, TILES)
                if c % 2 == 0:
                    pe.wait_ge(qx_in, nth(b, 512, 128 * (g + 1)))
                    pe.wait_ge(kl_ok, nth(b, GROUPS, g + 1))
                by_head = lambda ap: ap.rearrange("p (h n) -> p h n", h=HEADS)
                k0, q0 = GRP * (g % 2) + P * (c % 2), P * (c % 2)
                wins = [(slice(WIN * w, WIN * w + WIN), slice(k0 + WIN * w, k0 + WIN * w + WIN), q0 + WIN * w) for w in range(n)]
                for j in range(FOUR):
                    for r, kr, t0 in wins:
                        mm(by_head(D[r, 0:SW])[:, :, j:WIN:FOUR], ki[:, j, kr], x[:, :, t0 + j:t0 + WIN:FOUR], start=True, stop=True)
                for j in range(1, NE):
                    for r, kr, t0 in wins:
                        mm(by_head(D[r, SW:2 * SW])[:, :, EIGHT * j:EIGHT * j + EIGHT], ko[:, j - 1, kr],
                           x[:, :, Q8 + t0 + EIGHT * j:Q8 + t0 + EIGHT * j + EIGHT], start=True, stop=True)
                for r, kr, t0 in wins:
                    last = mm(by_head(D[r, 2 * SW:2 * SW + SW // 2]), kh[:, kr], x[:, :, Q4 + t0 // 2:Q4 + t0 // 2 + WIN // 2],
                              start=True, stop=True)
                last.then_inc(diag, 1)
                if c:
                    pe.wait_ge(px_ok, nth(b, TILES, c))
                else:
                    before(pe, px_ok, b, TILES, TILES)
                for w in range(1, n):
                    rows = WIN * w if w < 3 else P
                    last = mm(by_head(O[0:rows, SW * (w - 1):SW * w]), kw[:, w - 1, k0:k0 + rows],
                              x[:, :, Q32 + q0 + WIN * w:Q32 + q0 + WIN * w + WIN], start=True, stop=True)
                last.then_inc(off, 1)

            def scan(b, c):
                n, s0, S = WIN * windows[c], P * (c % 4), bank[SOUT]
                if c == 0:
                    before(pe, ga_ok, b, 2, 2)
                    pe.wait_ge(v_in, nth(b, 16, 16))
                if c == 4:
                    pe.wait_ge(ga_ok, nth(b, 2, 1))
                if c == 1:
                    pe.wait_ge(ab_ok, nth(b, 1, 1))
                    pe.wait_ge(qc_ok, nth(b, 1, 1))
                if c:
                    mm(S[:, s0:s0 + n], ab[:, c - 1, :], qc[:, P * c:P * c + n], start=True, stop=False, skip_group_check=True)
                pe.wait_ge(px_ok, nth(b, TILES, c + 1))
                for hd in range(HEADS):
                    r = slice(HD * hd, HD * hd + HD)
                    last = mm(S[r, s0:s0 + n], v[:, c, r], px[c % 2][:, hd, 0:n], start=(c == 0), stop=True, skip_group_check=True)
                last.then_inc(s_out, 1)

            def attends(p, g):
                bk = rest_bank(pe, p, f"wo{g}")
                pe.wait_ge(ga_ok, nth(p, 2, g + 1))
                product(bk, ga, wo, g).then_inc(rest, 1)

            def n2Ts(p, g):
                bk = rest_bank(pe, p, f"n2T{g}")
                pe.wait_ge(nl2_ok, nth(p, 2, g + 1))
                transposed(bk, lambda m: nl2[:, m, :], tiles(g)).then_inc(rest, 1)

            def w1s(p, g):
                pe.wait_ge(n2T_ok, nth(p, 2, g + 1))
                for j in range(4):
                    bk = rest_bank(pe, p, f"w1_{g}{j}")
                    mm(bk[:, 0:width[g]], w1[:, P * j:P * j + P], c1[:, cols(g)], start=True, stop=True).then_inc(rest, 1)

            def w2s(p, g):
                bk = rest_bank(pe, p, f"w2_{g}")
                pe.wait_ge(ge1, nth(p, 8, 4 * g + 4))
                for i, m in enumerate(tiles(g)):
                    for j in range(4):
                        last = mm(bk[:, P * i:P * i + P], hid[:, j, P * m:P * m + P], w2[:, j, :], start=(j == 0), stop=(j == 3))
                last.then_inc(rest, 1)

            def nTT(p, g):
                bk = rest_bank(pe, p, f"n1T{g}")
                pe.wait_ge(n12_ok, nth(p, 2, g + 1))
                transposed(bk, lambda m: n1[:, m, :], tiles(g)).then_inc(rest, 1)
                bk = rest_bank(pe, p, f"nmT{g}")
                transposed(bk, lambda m: n2[:, m, :], tiles(g)).then_inc(rest, 1)

            def ats(p, g):
                bk = rest_bank(pe, p, f"at{g}")
                pe.wait_ge(nmT_ok, nth(p, 2, g + 1))
                mm(bk[:, 0:width[g]], wat[:, :], c1[:, cols(g)], start=True, stop=True).then_inc(rest, 1)

            def f1s(p, g):
                pe.wait_ge(xa_ok, nth(p, 2, g + 1))
                pe.wait_ge(e_in, nth(p, 48, 48))
                for j in range(4):
                    bk = rest_bank(pe, p, f"f1_{g}{j}")
                    mm(bk[:, 0:width[g]], f1w[:, P * j:P * j + P], xa[:, cols(g)], start=True, stop=True).then_inc(rest, 1)

            def f2s(p, g):
                bk = rest_bank(pe, p, f"f2_{g}")
                for j in range(4):
                    pe.wait_ge(ge2, nth(p, 8, 4 * g + j + 1))
                    last = mm(bk[:, 0:width[g]], f2w[:, P * j:P * j + P], hid[:, j, cols(g)], start=(j == 0), stop=(j == 3))
                last.then_inc(rest, 1)

            def oTs(p, g):
                bk = rest_bank(pe, p, f"oT{g}")
                pe.wait_ge(fin_ok, nth(p, 2, g + 1))
                transposed(bk, lambda m: c1[:, P * m:P * m + P], tiles(g)).then_inc(rest, 1)

            def body(f, s, m, t):
                if s is not None:
                    pairs(s, 0); rTs(s, 0); rTs(s, 1)
                if t is not None:
                    oTs(t, 0)
                if f is not None:
                    dcts(f, 0); dcts(f, 1)
                if t is not None:
                    f1s(t, 1); f2s(t, 1)
                if s is not None:
                    pairs(s, 1); scan(s, 0)
                if f is not None:
                    nTs(f, 0); nTs(f, 1)
                if t is not None:
                    oTs(t, 1)
                if m is not None:
                    attends(m, 0); attends(m, 1)
                if s is not None:
                    pairs(s, 2); scan(s, 1)
                if f is not None:
                    qkv(f, "q", 0); qkv(f, "q", 1)
                if m is not None:
                    n2Ts(m, 0)
                if f is not None:
                    qkv(f, "k", 0); qkv(f, "k", 1)
                if m is not None:
                    n2Ts(m, 1); w1s(m, 0)
                if s is not None:
                    pairs(s, 3); scan(s, 2)
                if m is not None:
                    w1s(m, 1)
                if f is not None:
                    qkv(f, "v", 0); qkv(f, "v", 1)
                if s is not None:
                    pairs(s, 4); scan(s, 3)
                if f is not None:
                    qkTs(f, 0, 0); qkTs(f, 0, 1)
                if m is not None:
                    w2s(m, 0)
                if s is not None:
                    pairs(s, 5); scan(s, 4)
                if f is not None:
                    qkTs(f, 1, 0); qkTs(f, 1, 1)
                if m is not None:
                    w2s(m, 1)
                if s is not None:
                    pairs(s, 6); scan(s, 5)
                if f is not None:
                    gates(f, 0); gates(f, 1); kcs(f, 0); kcs(f, 1)
                if m is not None:
                    nTT(m, 0); nTT(m, 1); ats(m, 0); ats(m, 1); f1s(m, 0)
                if s is not None:
                    pairs(s, 7); scan(s, 6)
                if f is not None:
                    us(f)
                if m is not None:
                    f2s(m, 0)
                if f is not None:
                    zts(f)
                if s is not None:
                    scan(s, 7)
            rounds(pe, body)


def kernel(**inputs):
    import numpy as np
    import concourse.bacc as bacc
    from concourse.bass_utils import run_bass_kernel_spmd

    I = {n: np.asarray(a) for n, a in inputs.items()}
    at = lambda n: I["L0_attn_" + n]
    ff = lambda n: I["L0_ffn_" + n]
    C = np.ascontiguousarray
    x = I["x"]
    full = x.shape[1] // P
    hd = np.arange(P) // HD
    arrays = {
        "xT": C(x[:, :full * P].reshape(x.shape[0], full, P).transpose(0, 2, 1)),
        "xtail": C(x[:, full * P:]),
        "ident": np.eye(P, dtype=np.float32),
        "heads1": (hd[:, None] == hd[None, :]).astype(np.float32),
        "dct": dct_basis(), "mask": pair_mask(),
        "wqT": C(at("Wq").T), "wkT": C(at("Wk").T), "wvT": C(at("Wv").T), "wgT": C(at("Wg").T),
        "woT": C(at("Wo").T), "w1T": C(at("W1").T), "w2T": C(at("W2").T),
        "watT": C(ff("attn_w").T), "wnextT": C(ff("next_w").T),
        "fc1T": C(ff("fc1_w").transpose(0, 2, 1)), "fc2": C(ff("fc2_w")),
        "fc1b": C(ff("fc1_b").reshape(-1, 4, P).transpose(0, 2, 1)), "fc2bT": C(ff("fc2_b").T),
        "vec": np.stack([at("ln1_g"), at("ln1_b"), at("ln2_g"), at("ln2_b"), at("time_decay"),
                         at("tm_q").reshape(-1), at("tm_k").reshape(-1), at("tm_v").reshape(-1), at("tm_g").reshape(-1),
                         at("rms_scale"), ff("ln_g"), ff("ln_b"), ff("attn_b"), ff("next_b")], axis=1),
    }
    arrays = {n: C(a) for n, a in arrays.items()}
    nc = bacc.Bacc("TRN2", target_bir_lowering=False, num_devices=1)
    aps = {n: nc.dram_tensor(f"in_{n}", a.shape, mybir.dt.from_np(a.dtype), kind="ExternalInput").ap()
           for n, a in arrays.items()}
    out = nc.dram_tensor("out_0", (x.shape[0], full + 1, P), F32, kind="ExternalOutput").ap()
    program(nc, aps, out)
    r = run_bass_kernel_spmd(nc, [{f"in_{n}": a for n, a in arrays.items()}], core_ids=[0])
    return r.results[0]["out_0"]
```
